# Optimizing a Trainium2 kernel written in Bass

```python
import numpy as np
import jax
import jax.numpy as jnp

def _softmax(x, axis=-1):
    return jax.nn.softmax(x, axis=axis)

def _gelu(x):
    return jax.nn.gelu(x, approximate=True)

def _silu(x):
    return jax.nn.silu(x)

def _sigmoid(x):
    return jax.nn.sigmoid(x)

def _layernorm(x, axis=-1, eps=1e-05):
    m = jnp.mean(x, axis=axis, keepdims=True)
    v = jnp.var(x, axis=axis, keepdims=True)
    return (x - m) / jnp.sqrt(v + eps)

def _scatter_add(tgt, idx, src, axis=0):
    return tgt.at[idx].add(src)

def _segment_sum(src, seg, n):
    return jax.ops.segment_sum(src, seg, n)
kernel_name = 'mk_seq_preln_d1_jaxref_r4_7795d9'

def setup_inputs(seed: int=0):
    np.random.seed(seed)
    _w = jnp.asarray

    def _L0_attn_setup():
        import jax, jax.numpy as jnp
        import numpy as np
        EMB = 256
        H = 16
        D = EMB // H
        EPS = 1e-05
        SM_SCALE = 1.0
        CAUSAL = True
        NEG = -1e+30

        def _layernorm(t, g, b):
            m = jnp.mean(t, axis=-1, keepdims=True)
            v = jnp.mean(jnp.square(t - m), axis=-1, keepdims=True)
            return (t - m) * jax.lax.rsqrt(v + EPS) * g + b
        key = jax.random.key(seed)
        ks = jax.random.split(key, 8)
        N, L = (2, 512)
        x = jax.random.normal(ks[0], (N, L, EMB), dtype=jnp.float32)
        mask = jnp.ones((N, L), dtype=jnp.int32)
        s = 0.02
        Wq = jax.random.normal(ks[1], (EMB, EMB), dtype=jnp.float32) * s
        Wk = jax.random.normal(ks[2], (EMB, EMB), dtype=jnp.float32) * s
        Wv = jax.random.normal(ks[3], (EMB, EMB), dtype=jnp.float32) * s
        Wo = jax.random.normal(ks[4], (EMB, EMB), dtype=jnp.float32) * s
        bo = jnp.zeros((EMB,), dtype=jnp.float32)
        gq = jnp.ones((D,), dtype=jnp.float32)
        bq = jnp.zeros((D,), dtype=jnp.float32)
        gk = jnp.ones((D,), dtype=jnp.float32)
        bk = jnp.zeros((D,), dtype=jnp.float32)
        return {'x': x, 'mask': mask, 'Wq': Wq, 'Wk': Wk, 'Wv': Wv, 'gq': gq, 'bq': bq, 'gk': gk, 'bk': bk, 'Wo': Wo, 'bo': bo}
    _L0_attn_in = _L0_attn_setup()

    def _L0_ffn_setup():
        import jax, jax.numpy as jnp
        import numpy as np
        B, T, C = (2, 512, 256)
        H, D = (16, 64)
        CR = 8
        R = C // CR
        ROPE = D // 2
        NOPE = D - ROPE
        E, K, I, S = (8, 2, 128, 1)
        THETA = 100000.0
        EPS = 1e-05

        def _rmsnorm(x, w):
            rms = jnp.sqrt(jnp.mean(x * x, axis=-1, keepdims=True) + EPS)
            return w * (x / rms)

        def _rope(xh):
            d = xh.shape[-1]
            t = jnp.arange(xh.shape[2], dtype=jnp.float32)
            freqs = 1.0 / THETA ** (jnp.arange(0, d, 2, dtype=jnp.float32) / d)
            ang = jnp.outer(t, freqs)
            cos, sin = (jnp.cos(ang), jnp.sin(ang))
            xr = xh.reshape(xh.shape[:-1] + (d // 2, 2))
            x0, x1 = (xr[..., 0], xr[..., 1])
            rot = jnp.stack([x0 * cos - x1 * sin, x0 * sin + x1 * cos], axis=-1)
            return rot.reshape(xh.shape)

        def _attention(x, Wq, Wkva, Wkvb, Wo):
            b, t, _ = x.shape
            q = (x @ Wq).reshape(b, t, H, D).transpose(0, 2, 1, 3)
            ckv = x @ Wkva
            kv_latent, k_rope = (ckv[:, :, :R], ckv[:, :, R:])
            kv = (kv_latent @ Wkvb).reshape(b, t, H, NOPE).transpose(0, 2, 1, 3)
            k_rope = jnp.broadcast_to(k_rope[:, None, :, :], (b, H, t, ROPE))
            q_nope, q_rope = (q[..., :NOPE], q[..., NOPE:])
            q = jnp.concatenate([q_nope, _rope(q_rope)], axis=-1)
            k = jnp.concatenate([kv, _rope(k_rope)], axis=-1)
            v = jnp.concatenate([kv, jnp.zeros_like(k_rope)], axis=-1)
            att = jnp.einsum('bhqd,bhkd->bhqk', q, k) / jnp.sqrt(jnp.float32(D))
            mask = jnp.tril(jnp.ones((t, t), dtype=bool))
            att = jnp.where(mask, att, jnp.float32(-jnp.inf))
            att = jax.nn.softmax(att, axis=-1)
            y = jnp.einsum('bhqk,bhkd->bhqd', att, v)
            y = y.transpose(0, 2, 1, 3).reshape(b, t, H * D)
            return y @ Wo

        def _experts(x_flat, Wg, Wu, Wd):
            g = jax.nn.silu(jnp.einsum('nc,eci->nei', x_flat, Wg))
            u = jnp.einsum('nc,eci->nei', x_flat, Wu)
            return jnp.einsum('nei,eic->nec', g * u, Wd)

        def _moe(x, Wgate, expert_bias, Wg, Wu, Wd, sWg, sWu, sWd):
            b, t, c = x.shape
            xf = x.reshape(-1, c)
            shared = jnp.mean(_experts(xf, sWg, sWu, sWd), axis=1)
            logits = xf @ Wgate + expert_bias
            probs = jax.nn.softmax(logits, axis=-1)
            topk_p, topk_i = jax.lax.top_k(probs, K)
            topk_p = topk_p / jnp.sum(topk_p, axis=-1, keepdims=True)
            comb = jnp.sum(jax.nn.one_hot(topk_i, E, dtype=xf.dtype) * topk_p[..., None], axis=1)
            routed = jnp.einsum('ne,nec->nc', comb, _experts(xf, Wg, Wu, Wd))
            return (shared + routed).reshape(b, t, c)
        key = jax.random.key(seed)
        ks = jax.random.split(key, 16)
        w = lambda k, shp: jax.random.normal(k, shp, dtype=jnp.float32) * 0.02
        return {'x': jax.random.normal(ks[0], (B, T, C), dtype=jnp.float32), 'w_ln1': jnp.ones((C,), jnp.float32), 'Wq': w(ks[1], (C, H * D)), 'Wkva': w(ks[2], (C, R + ROPE)), 'Wkvb': w(ks[3], (R, H * NOPE)), 'Wo': w(ks[4], (H * D, C)), 'w_ln2': jnp.ones((C,), jnp.float32), 'Wgate': w(ks[5], (C, E)), 'expert_bias': jnp.zeros((E,), jnp.float32), 'Wg': w(ks[6], (E, C, I)), 'Wu': w(ks[7], (E, C, I)), 'Wd': w(ks[8], (E, I, C)), 'sWg': w(ks[9], (S, C, I)), 'sWu': w(ks[10], (S, C, I)), 'sWd': w(ks[11], (S, I, C))}
    _L0_ffn_in = _L0_ffn_setup()
    _d = {'L0_attn_x': _L0_attn_in['x'], 'L0_attn_mask': _L0_attn_in['mask'], 'L0_attn_Wq': _L0_attn_in['Wq'], 'L0_attn_Wk': _L0_attn_in['Wk'], 'L0_attn_Wv': _L0_attn_in['Wv'], 'L0_attn_gq': _L0_attn_in['gq'], 'L0_attn_bq': _L0_attn_in['bq'], 'L0_attn_gk': _L0_attn_in['gk'], 'L0_attn_bk': _L0_attn_in['bk'], 'L0_attn_Wo': _L0_attn_in['Wo'], 'L0_attn_bo': _L0_attn_in['bo'], 'L0_ffn_w_ln1': _L0_ffn_in['w_ln1'], 'L0_ffn_Wq': _L0_ffn_in['Wq'], 'L0_ffn_Wkva': _L0_ffn_in['Wkva'], 'L0_ffn_Wkvb': _L0_ffn_in['Wkvb'], 'L0_ffn_Wo': _L0_ffn_in['Wo'], 'L0_ffn_w_ln2': _L0_ffn_in['w_ln2'], 'L0_ffn_Wgate': _L0_ffn_in['Wgate'], 'L0_ffn_expert_bias': _L0_ffn_in['expert_bias'], 'L0_ffn_Wg': _L0_ffn_in['Wg'], 'L0_ffn_Wu': _L0_ffn_in['Wu'], 'L0_ffn_Wd': _L0_ffn_in['Wd'], 'L0_ffn_sWg': _L0_ffn_in['sWg'], 'L0_ffn_sWu': _L0_ffn_in['sWu'], 'L0_ffn_sWd': _L0_ffn_in['sWd']}
    _x0 = _d['L0_attn_x']
    _d['L0_attn_x'] = jax.random.normal(jax.random.fold_in(jax.random.key(seed), 1), (16, 512, 256), dtype=_x0.dtype)
    del _x0
    return _d

def reference(L0_attn_x, L0_attn_mask, L0_attn_Wq, L0_attn_Wk, L0_attn_Wv, L0_attn_gq, L0_attn_bq, L0_attn_gk, L0_attn_bk, L0_attn_Wo, L0_attn_bo, L0_ffn_w_ln1, L0_ffn_Wq, L0_ffn_Wkva, L0_ffn_Wkvb, L0_ffn_Wo, L0_ffn_w_ln2, L0_ffn_Wgate, L0_ffn_expert_bias, L0_ffn_Wg, L0_ffn_Wu, L0_ffn_Wd, L0_ffn_sWg, L0_ffn_sWu, L0_ffn_sWd):

    def _L0_attn_ref(x, mask, Wq, Wk, Wv, gq, bq, gk, bk, Wo, bo):
        import jax, jax.numpy as jnp
        import numpy as np
        EMB = 256
        H = 16
        D = EMB // H
        EPS = 1e-05
        SM_SCALE = 1.0
        CAUSAL = True
        NEG = -1e+30

        def _layernorm(t, g, b):
            m = jnp.mean(t, axis=-1, keepdims=True)
            v = jnp.mean(jnp.square(t - m), axis=-1, keepdims=True)
            return (t - m) * jax.lax.rsqrt(v + EPS) * g + b
        N, L, _ = x.shape
        q = (x @ Wq.T).reshape(N, L, H, D).transpose(0, 2, 1, 3)
        k = (x @ Wk.T).reshape(N, L, H, D).transpose(0, 2, 1, 3)
        v = (x @ Wv.T).reshape(N, L, H, D).transpose(0, 2, 1, 3)
        q = _layernorm(q, gq, bq)
        k = _layernorm(k, gk, bk)
        scores = jnp.einsum('nhld,nhmd->nhlm', q, k) * SM_SCALE
        if CAUSAL:
            causal = jnp.tril(jnp.ones((L, L), dtype=bool))
            scores = jnp.where(causal, scores, NEG)
        attn = jax.nn.softmax(scores, axis=-1)
        out = jnp.einsum('nhlm,nhmd->nhld', attn, v)
        out = out.transpose(0, 2, 1, 3).reshape(N, L, EMB)
        return out @ Wo.T + bo

    def _L0_ffn_ref(x, w_ln1, Wq, Wkva, Wkvb, Wo, w_ln2, Wgate, expert_bias, Wg, Wu, Wd, sWg, sWu, sWd):
        import jax, jax.numpy as jnp
        import numpy as np
        B, T, C = (2, 512, 256)
        H, D = (16, 64)
        CR = 8
        R = C // CR
        ROPE = D // 2
        NOPE = D - ROPE
        E, K, I, S = (8, 2, 128, 1)
        THETA = 100000.0
        EPS = 1e-05

        def _rmsnorm(x, w):
            rms = jnp.sqrt(jnp.mean(x * x, axis=-1, keepdims=True) + EPS)
            return w * (x / rms)

        def _rope(xh):
            d = xh.shape[-1]
            t = jnp.arange(xh.shape[2], dtype=jnp.float32)
            freqs = 1.0 / THETA ** (jnp.arange(0, d, 2, dtype=jnp.float32) / d)
            ang = jnp.outer(t, freqs)
            cos, sin = (jnp.cos(ang), jnp.sin(ang))
            xr = xh.reshape(xh.shape[:-1] + (d // 2, 2))
            x0, x1 = (xr[..., 0], xr[..., 1])
            rot = jnp.stack([x0 * cos - x1 * sin, x0 * sin + x1 * cos], axis=-1)
            return rot.reshape(xh.shape)

        def _attention(x, Wq, Wkva, Wkvb, Wo):
            b, t, _ = x.shape
            q = (x @ Wq).reshape(b, t, H, D).transpose(0, 2, 1, 3)
            ckv = x @ Wkva
            kv_latent, k_rope = (ckv[:, :, :R], ckv[:, :, R:])
            kv = (kv_latent @ Wkvb).reshape(b, t, H, NOPE).transpose(0, 2, 1, 3)
            k_rope = jnp.broadcast_to(k_rope[:, None, :, :], (b, H, t, ROPE))
            q_nope, q_rope = (q[..., :NOPE], q[..., NOPE:])
            q = jnp.concatenate([q_nope, _rope(q_rope)], axis=-1)
            k = jnp.concatenate([kv, _rope(k_rope)], axis=-1)
            v = jnp.concatenate([kv, jnp.zeros_like(k_rope)], axis=-1)
            att = jnp.einsum('bhqd,bhkd->bhqk', q, k) / jnp.sqrt(jnp.float32(D))
            mask = jnp.tril(jnp.ones((t, t), dtype=bool))
            att = jnp.where(mask, att, jnp.float32(-jnp.inf))
            att = jax.nn.softmax(att, axis=-1)
            y = jnp.einsum('bhqk,bhkd->bhqd', att, v)
            y = y.transpose(0, 2, 1, 3).reshape(b, t, H * D)
            return y @ Wo

        def _experts(x_flat, Wg, Wu, Wd):
            g = jax.nn.silu(jnp.einsum('nc,eci->nei', x_flat, Wg))
            u = jnp.einsum('nc,eci->nei', x_flat, Wu)
            return jnp.einsum('nei,eic->nec', g * u, Wd)

        def _moe(x, Wgate, expert_bias, Wg, Wu, Wd, sWg, sWu, sWd):
            b, t, c = x.shape
            xf = x.reshape(-1, c)
            shared = jnp.mean(_experts(xf, sWg, sWu, sWd), axis=1)
            logits = xf @ Wgate + expert_bias
            probs = jax.nn.softmax(logits, axis=-1)
            topk_p, topk_i = jax.lax.top_k(probs, K)
            topk_p = topk_p / jnp.sum(topk_p, axis=-1, keepdims=True)
            comb = jnp.sum(jax.nn.one_hot(topk_i, E, dtype=xf.dtype) * topk_p[..., None], axis=1)
            routed = jnp.einsum('ne,nec->nc', comb, _experts(xf, Wg, Wu, Wd))
            return (shared + routed).reshape(b, t, c)
        x = x + _attention(_rmsnorm(x, w_ln1), Wq, Wkva, Wkvb, Wo)
        residual = x
        xn = _rmsnorm(x, w_ln2)
        x_out = _moe(xn, Wgate, expert_bias, Wg, Wu, Wd, sWg, sWu, sWd)
        return residual + x_out
    x = L0_attn_x
    x = x + _L0_attn_ref(_layernorm(x, axis=-1), L0_attn_mask, L0_attn_Wq, L0_attn_Wk, L0_attn_Wv, L0_attn_gq, L0_attn_bq, L0_attn_gk, L0_attn_bk, L0_attn_Wo, L0_attn_bo)
    x = x + _L0_ffn_ref(_layernorm(x, axis=-1), L0_ffn_w_ln1, L0_ffn_Wq, L0_ffn_Wkva, L0_ffn_Wkvb, L0_ffn_Wo, L0_ffn_w_ln2, L0_ffn_Wgate, L0_ffn_expert_bias, L0_ffn_Wg, L0_ffn_Wu, L0_ffn_Wd, L0_ffn_sWg, L0_ffn_sWu, L0_ffn_sWd)
    return x

_drawn_inputs = setup_inputs


def setup_inputs(seed=0):
    import zlib

    import numpy as np

    out = dict(_drawn_inputs(seed))
    spreads = {'L0_attn_gq': (1.0, 0.6),
     'L0_attn_bq': (0.0, 0.8),
     'L0_attn_gk': (1.0, 0.6),
     'L0_attn_bk': (0.0, 0.8),
     'L0_attn_bo': (0.0, 0.1),
     'L0_ffn_w_ln1': (1.0, 0.6),
     'L0_ffn_w_ln2': (1.0, 0.6),
     'L0_ffn_expert_bias': (0.0, 0.8)}
    factors = {'L0_ffn_Wq': 8.0,
     'L0_ffn_Wkva': 8.0,
     'L0_ffn_Wkvb': 8.0,
     'L0_ffn_Wo': 8.0,
     'L0_ffn_Wgate': 8.0,
     'L0_ffn_Wg': 8.0,
     'L0_ffn_Wu': 8.0,
     'L0_ffn_Wd': 8.0,
     'L0_ffn_sWg': 8.0,
     'L0_ffn_sWu': 8.0,
     'L0_ffn_sWd': 8.0}
    for name, (base, spread) in spreads.items():
        noise = np.random.default_rng([zlib.crc32(name.encode()), seed]).standard_normal(out[name].shape)
        drawn = base * np.exp(spread * noise) if base else spread * noise
        out[name] = jnp.asarray(drawn.astype(out[name].dtype))
    for name, factor in factors.items():
        out[name] = (out[name] * factor).astype(out[name].dtype)
    return out
```

```python
from contextlib import ExitStack

import numpy as np

import concourse.bass as bass
from concourse import mybir

F32 = mybir.dt.float32
F32R = mybir.dt.float32r
BF16 = mybir.dt.bfloat16
ALU = mybir.AluOpType
ACT = mybir.ActivationFunctionType
AX = mybir.AxisListType

P = 128
NB, L, C = 16, 512, 256
NT = L // P
KC = C // P
H = 16
D = C // H
HP = 32
G = 4
NG = H // G
SPLITS = 6
SD = SPLITS * D
R = 32
DK = 2 * R
E, I = 8, 128
NE = E + 1
EPS = 1e-5
UNITS = NG * NT
BLOCKS = NG * NT * (NT + 1) // 2

ACT_COPIES = (False,) * 8 + (True, True)


def acts(n):
    return ACT_COPIES[n % len(ACT_COPIES)]


def act_count(n):
    return sum(acts(i) for i in range(n))


ACT_BLOCKS = act_count(BLOCKS)
DVE_BLOCKS = BLOCKS - ACT_BLOCKS


ORDER = (0, 1, 2, 3)


def tile_of(u):
    return ORDER[u % NT]


def first_block(u):
    return u // NT * NT * (NT + 1) // 2 + sum(j + 1 for j in ORDER[:u % NT])


class Signal:

    def __init__(self, sem, per_batch):
        self.sem, self.per_batch = sem, per_batch

    def at(self, b, n):
        return b * self.per_batch + n


def build(nc, t):
    ctx = ExitStack()
    with ctx:
        _build(nc, ctx, t)


def _build(nc, ctx, dram):
    base = (nc.sbuf_base + 63) // 64 * 64
    place = [base]

    def at(name, shape, dt, offset):
        return nc.alloc_sbuf_tensor_at(name, shape, dt, offset=offset)

    def size(shape, dt):
        n = 2 if dt == BF16 else 4
        for s in shape[1:]:
            n *= s
        return (n + 63) // 64 * 64

    def new(name, shape, dt):
        x = at(name, shape, dt, place[0])
        place[0] += size(shape, dt)
        return x

    wqkv = new("wqkv", [P, 2, KC, 3 * C], F32R)
    woa = new("woa", [P, 2, NG, C], F32R)
    wq2 = new("wq2", [P, 2, KC, H * DK], F32R)
    wkv = new("wkv", [P, 2, KC, 3 * R], F32R)
    wob = new("wob", [P, 2, NG, C], F32R)
    wgu = new("wgu", [P, 2, NE, KC, 2 * I], F32R)
    wd = new("wd", [P, 2, NE, C], F32R)
    wgate = new("wgate", [P, 2, KC, E], F32R)
    ident = new("ident", [P, P], F32)
    ident16 = new("ident16", [P, P], BF16)
    mask16 = new("mask16", [P, P], BF16)
    cosq = new("cosq", [P, NT, R], F32)
    sinq = new("sinq", [P, NT, R], F32)
    coskt = new("coskt", [P, L], F32)
    gam = new("gam", [P, 2, D], F32)
    bet = new("bet", [P, 2, D], F32)
    bo = new("bo", [P, C], F32)
    ebias = new("ebias", [P, E], F32)
    below = new("below", [P, E, E], F32)
    expo = new("expo", [P, NT], F32)
    stats = new("stats", [P, 3, NT, 6], F32)
    mv = new("mv", [P, 3, NT, 2], F32)
    var = new("var", [P, 3, 2, NT], F32)
    rstd = new("rstd", [P, 3, 2, NT], F32)
    ssq = new("ssq", [P, 2, 2 * H], F32)
    lnv = new("lnv", [P, 2, 2 * H], F32)
    rq = new("rq", [P, 2, 4, 2 * H], F32)
    negmax = new("negmax", [P, 2, UNITS, G], F32)
    sums = new("sums", [P, 2, UNITS, G], F32)
    rsum = new("rsum", [P, 2, UNITS, G], F32)
    lg = new("lg", [P, NT, E], F32)
    lmax = new("lmax", [P, NT], F32)
    lsh = new("lsh", [P, NT, E], F32)
    pexp = new("pexp", [P, NT, E], F32)
    cmp1 = new("cmp1", [P, NT, E, E], F32)
    cmp2 = new("cmp2", [P, NT, E, E], F32)
    rank = new("rank", [P, NT, E], F32)
    chosen = new("chosen", [P, NT, E], F32)
    den = new("den", [P, NT], F32)
    rden = new("rden", [P, NT], F32)
    comb = new("comb", [P, NT, E], F32)

    arena = place[0]
    x_in = new("x_in", [P, NT, C], F32)
    x1 = new("x1", [P, NT, C], F32)
    xp = new("xp", [P, NT, C], F32)
    region_x = place[0]
    xn = new("xn", [P, NT, C], F32)
    xth = new("xth", [P, KC, L], F32R)
    xtl = new("xtl", [P, KC, L], F32R)
    place[0] += 4096
    oth = at("oth", [P, NG, L], F32R, region_x)
    otl = at("otl", [P, NG, L], F32R, region_x + 8192)
    region_q = place[0]
    qkt = new("qkt", [SD, 2 * H, L], BF16)
    qt = at("qt", [P, H, L], F32R, region_q)
    sg = at("sg", [P, 2, L], F32, region_q)
    hid = at("hid", [P, 2, L], F32, region_q + 4096)
    hidh = at("hidh", [P, 2, L], F32R, region_q + 8192)
    hidl = at("hidl", [P, 2, L], F32R, region_q + 12288)
    region_p = place[0]
    prob = new("prob", [P, 2, G, L], F32)
    probt = new("probt", [P, 2, NT, L], F32)
    o = region_p
    sq = at("sq", [P, 2, 2 * C], F32, o)
    qn = at("qn", [P, 2, 2 * C], F32, o + 4096)
    res1 = at("res1", [P, 2, 2 * C], F32, o + 8192)
    stk = at("stk", [P, 2, 2 * H, SPLITS, D], BF16, o + 12288)
    kf = at("kf", [P, L], F32, o)
    ka = at("ka", [P, L], F32, o + 2048)
    kb = at("kb", [P, L], F32, o + 4096)
    qf = at("qf", [P, 2, 8, DK], F32, o + 8192)
    ta = at("ta", [P, 2, 8, R], F32, o + 12288)
    tb = at("tb", [P, 2, 8, R], F32, o + 14336)
    stq = at("stq", [P, 2, 8, 2, DK], F32R, o + 16384)
    va = new("va", [P, NT, H, HP], F32)
    khh = new("khh", [P, L], F32R)
    kll = new("kll", [P, L], F32R)
    vb = new("vb", [P, NT, R], F32)
    osb = new("osb", [P, L], F32)
    onm = new("onm", [P, L], F32)
    rexp = new("rexp", [P, NT, G, HP], F32)
    assert place[0] <= nc.sbuf_usable_end, place[0]

    place[0] = arena
    r_qkv = new("r_qkv", [P, KC, 3 * C], F32)
    r_woa = new("r_woa", [P, NG, C], F32)
    r_wqt = new("r_wqt", [R, H, C], F32)
    r_wqr = new("r_wqr", [P, KC, H, R], F32)
    r_kvbt = new("r_kvbt", [R, H, R], F32)
    r_wob = new("r_wob", [R, H, C], F32)
    r_wq2 = new("r_wq2", [P, KC, H, DK], F32)
    r_kva = new("r_kva", [P, KC, 3 * R], F32)
    r_wobf = new("r_wobf", [P, NG, C], F32)
    r_gu = new("r_gu", [P, NE, KC, 2 * I], F32)
    r_d = new("r_d", [P, NE, C], F32)
    r_gate = new("r_gate", [P, KC, E], F32)
    r_ln = new("r_ln", [P, 2, KC], F32)
    r_sum = new("r_sum", [P, KC, 2 * H], F32)
    assert place[0] <= nc.sbuf_usable_end, place[0]

    scores = ctx.enter_context(nc.psum_tensor("scores", [P, 4, 512], F32))
    bank = [scores[:, i] for i in range(4)]
    bank += [ctx.enter_context(nc.psum_tensor(f"bank{i}", [P, 512], F32))[:, :] for i in range(4, 8)]

    def sem(name):
        return ctx.enter_context(nc.semaphore(name))

    raw_loaded = sem("raw_loaded")
    zeroed = sem("zeroed")
    va_zeroed = sem("va_zeroed")
    folded_psum = sem("folded_psum")
    centred = sem("centred")
    scaled = sem("scaled")
    hi_ready = sem("hi_ready")
    weights_ready = sem("weights_ready")
    x_loaded = Signal(sem("x_loaded"), 16)
    out_stored = Signal(sem("out_stored"), 16)
    var_ready = Signal(sem("var_ready"), 4)
    rstd_ready = Signal(sem("rstd_ready"), 4)
    xn_ready = Signal(sem("xn_ready"), 3 * NT)
    xt_psum = Signal(sem("xt_psum"), 3 * KC)
    xth_ready = Signal(sem("xth_ready"), 3 * KC)
    xtl_ready = Signal(sem("xtl_ready"), 3 * KC)
    xb_ready = Signal(sem("xb_ready"), NT)
    qk_psum = Signal(sem("qk_psum"), NT)
    v_psum = Signal(sem("v_psum"), NT)
    sq_ready = Signal(sem("sq_ready"), NT)
    v_ready = Signal(sem("v_ready"), NT)
    ssq_ready = Signal(sem("ssq_ready"), NT)
    root_ready = Signal(sem("root_ready"), NT)
    rq_ready = Signal(sem("rq_ready"), NT)
    qn_ready = Signal(sem("qn_ready"), NT)
    qhat_ready = Signal(sem("qhat_ready"), NT)
    part1_ready = Signal(sem("part1_ready"), NT)
    stack_ready = Signal(sem("stack_ready"), NT)
    stackt_psum = Signal(sem("stackt_psum"), 4 * NT)
    stackt_act = Signal(sem("stackt_act"), 2 * NT)
    stackt_dve = Signal(sem("stackt_dve"), 2 * NT)
    kv_psum = Signal(sem("kv_psum"), 1)
    kv_copied = Signal(sem("kv_copied"), 1)
    kf_ready = Signal(sem("kf_ready"), 1)
    khh_ready = Signal(sem("khh_ready"), 1)
    kll_ready = Signal(sem("kll_ready"), 1)
    vb_psum = Signal(sem("vb_psum"), 1)
    vb_ready = Signal(sem("vb_ready"), 1)
    q_psum = Signal(sem("q_psum"), 2 * NT)
    nope_ready = Signal(sem("nope_ready"), 2 * NT)
    rot_ready = Signal(sem("rot_ready"), 2 * NT)
    rope_ready = Signal(sem("rope_ready"), 2 * NT)
    qh_ready = Signal(sem("qh_ready"), 2 * NT)
    ql_ready = Signal(sem("ql_ready"), 2 * NT)
    qt_psum = Signal(sem("qt_psum"), 4 * NT)
    qt_act = Signal(sem("qt_act"), 2 * NT)
    qt_dve = Signal(sem("qt_dve"), 2 * NT)
    s_psum = Signal(sem("s_psum"), 2 * 2 * UNITS)
    negmax_ready = Signal(sem("negmax_ready"), 2 * 2 * UNITS)
    prob_ready = Signal(sem("prob_ready"), 2 * G * UNITS)
    probt_psum = Signal(sem("probt_psum"), 2 * BLOCKS)
    probt_act = Signal(sem("probt_act"), 2 * ACT_BLOCKS)
    probt_dve = Signal(sem("probt_dve"), 2 * DVE_BLOCKS)
    pv_done = Signal(sem("pv_done"), 2 * UNITS)
    rsum_ready = Signal(sem("rsum_ready"), 2 * NG)
    rexp_ready = Signal(sem("rexp_ready"), 2 * NG)
    rsumt_psum = Signal(sem("rsumt_psum"), 2 * NG)
    osb_ready = Signal(sem("osb_ready"), 2 * NG)
    onm_ready = Signal(sem("onm_ready"), 2 * NG)
    oth_ready = Signal(sem("oth_ready"), 2 * NG)
    otl_ready = Signal(sem("otl_ready"), 2 * NG)
    y_psum = Signal(sem("y_psum"), 2 * NT)
    y_added = Signal(sem("y_added"), 2 * NT)
    gate_psum = Signal(sem("gate_psum"), 1)
    logits_ready = Signal(sem("logits_ready"), 1)
    pexp_ready = Signal(sem("pexp_ready"), 1)
    gate_up_psum = Signal(sem("gate_up_psum"), NE)
    silu_ready = Signal(sem("silu_ready"), NE)
    hid_ready = Signal(sem("hid_ready"), NE)
    hidh_ready = Signal(sem("hidh_ready"), NE)
    hidl_ready = Signal(sem("hidl_ready"), NE)
    down_psum = Signal(sem("down_psum"), 2 * NE)
    down_added = Signal(sem("down_added"), NE)
    dve_passed, pe_passed, pool_passed = sem("dve_passed"), sem("pe_passed"), sem("pool_passed")
    dve_link = sem("dve_link")
    pool_link = sem("pool_link")
    act_link = sem("act_link")
    DVE_LINKS, POOL_LINKS, ACT_LINKS = 31, 16, 4

    block = ctx.enter_context(nc.Block())

    def settle(eng, passed):
        eng.sem_inc(passed, 1)

    class Chain:

        def __init__(self, eng, semaphore, per_batch):
            self.eng, self.sem, self.per_batch, self.n = eng, semaphore, per_batch, 0

        def start(self, b):
            self.b, self.n = b, 0

        def link(self, ins):
            self.n += 1
            ins.then_inc(self.sem, 1)
            self.eng.wait_ge(self.sem, self.b * self.per_batch + self.n)

        def end(self):
            assert self.n == self.per_batch, (self.n, self.per_batch)

    def block_copied(b, a, n):
        if acts(n):
            return probt_act.sem, probt_act.at(b, a * ACT_BLOCKS + act_count(n + 1))
        return probt_dve.sem, probt_dve.at(b, a * DVE_BLOCKS + n + 1 - act_count(n + 1))

    XT = (xth, xtl)
    TERMS = ((0, 0), (0, 1), (1, 0))

    SPLIT = ((r_woa, woa, 0), (r_d, wd, 0), (r_qkv, wqkv, 1), (r_wq2, wq2, 2), (r_kva, wkv, 3), (r_wobf, wob, 4),
             (r_gu, wgu, 5), (r_gate, wgate, 6))

    def flat(x):
        s = [f"d{i}" for i in range(len(x.shape) - 1)]
        return x.rearrange(f"p {' '.join(s)} -> p ({' '.join(s)})")

    n_raw = [0]

    @block.sync
    def _(sp):
        def load(dst, src):
            sp.dma_start(dst, src).then_inc(raw_loaded, 16)
            n_raw[0] += 16

        for n, name in enumerate(("wq1t", "wk1t", "wv1t")):
            load(r_qkv[:, :, n * C:(n + 1) * C], dram[name].rearrange("(k p) n -> p k n", p=P))
        load(r_wqt[:, :, :], dram["wq2_nope_t"].rearrange("h j c -> j h c"))
        load(r_kvbt[:, :, :], dram["wkvb_t"].rearrange("h j r -> j h r"))
        for k in range(KC):
            load(r_wqr[:, k], dram["wq2"][k * P:(k + 1) * P].rearrange("p (h d) -> p h d", h=H)[:, :, R:DK])
        load(r_kva[:, :, 0:DK], dram["wkva"].rearrange("(k p) n -> p k n", p=P))
        load(r_wob[:, :, :], dram["wo2"].rearrange("(h d) n -> d h n", h=H)[0:R])
        for name, n in (("w_ln1", 0), ("w_ln2", 1)):
            for k in range(KC):
                load(r_ln[:, n, k:k + 1], dram[name][k * P:(k + 1) * P].rearrange("(p o) -> p o", o=1))
        for n, name in enumerate(("g", "u")):
            for k in range(KC):
                rows = slice(k * P, (k + 1) * P)
                load(r_gu[:, 0, k, n * I:(n + 1) * I], dram["sw" + name][0, rows])
                load(r_gu[:, 1:NE, k, n * I:(n + 1) * I], dram["w" + name][:, rows].rearrange("e p i -> p e i"))
        load(r_d[:, 0], dram["swd"][0])
        load(r_d[:, 1:NE], dram["wd"].rearrange("e i c -> i e c"))
        load(r_gate[:, :, :], dram["wgate"].rearrange("(k p) e -> p k e", p=P))
        load(ident[:, :], dram["ident"])
        load(ident16[:, :], dram["ident16"])
        load(mask16[:, :], dram["mask16"])
        load(below[:, :, :], dram["below"].rearrange("(o e) f -> o e f", o=1).to_broadcast([P, E, E]))
        load(cosq[:, :, :], dram["cos"].rearrange("(t p) r -> p t r", p=P))
        load(sinq[:, :, :], dram["sin"].rearrange("(t p) r -> p t r", p=P))
        load(coskt[R:2 * R], dram["cos_t"])
        load(coskt[2 * R:3 * R], dram["sin_t"])
        for n, (g_, b_) in enumerate((("gq", "bq"), ("gk", "bk"))):
            load(gam[:, n], dram[g_].rearrange("(o d) -> o d", o=1).to_broadcast([P, D]))
            load(bet[:, n], dram[b_].rearrange("(o d) -> o d", o=1).to_broadcast([P, D]))
        load(bo[:, :], dram["bo"].rearrange("(o d) -> o d", o=1).to_broadcast([P, C]))
        load(ebias[:, :], dram["ebias"].rearrange("(o d) -> o d", o=1).to_broadcast([P, E]))
        sp.wait_ge(zeroed, 1)
        for q in range(G):
            load(r_woa[q * HP:q * HP + D],
                 dram["wo1t"].rearrange("(g q d) n -> q d g n", q=G, d=D)[q])

        sp.sem_inc(out_stored.sem, 16)
        sp.wait_ge(weights_ready, len(SPLIT))
        sp.dma_start(x_in[:, :, :], dram["x"][0].rearrange("(t p) c -> p t c", p=P)).then_inc(x_loaded.sem, 16)
        with sp.Fori(0, NB - 1) as b:
            sp.wait_ge(y_added.sem, y_added.at(b, NT))
            sp.dma_start(x_in[:, :, :], dram["x_rows"][bass.ds(b * L + L, L)].rearrange("(t p) c -> p t c", p=P)).then_inc(x_loaded.sem, 16)
            sp.wait_ge(down_added.sem, down_added.at(b, NE))
            sp.dma_start(dram["out"][bass.ds(b * L, L)].rearrange("(t p) c -> p t c", p=P), x1[:, :, :]).then_inc(out_stored.sem, 16)
        sp.wait_ge(down_added.sem, down_added.at(NB - 1, NE))
        sp.dma_start(dram["out"][(NB - 1) * L:NB * L].rearrange("(t p) c -> p t c", p=P), x1[:, :, :]).then_inc(out_stored.sem, 16)
        sp.wait_ge(out_stored.sem, 16 * (NB + 1))

    @block.gpsimd
    def _(pool):
        chain = Chain(pool, pool_link, POOL_LINKS)
        nc.gpsimd.memset(r_woa[:, :, :], 0.0).then_inc(zeroed, 1)
        nc.gpsimd.memset(expo[:, :], -0.5)
        pool.wait_ge(weights_ready, len(SPLIT))
        nc.gpsimd.memset(va[:, :, :, :], 0.0).then_inc(va_zeroed, 1)
        pool.wait_ge(va_zeroed, 1)

        with pool.Fori(0, NB) as b:
            chain.start(b)

            def root(stage, n, count):
                pool.wait_ge(var_ready.sem, var_ready.at(b, count))
                nc.gpsimd.tensor_tensor(rstd[:, stage, n], var[:, stage, n], expo[:, :], ALU.pow).then_inc(rstd_ready.sem, 1)

            def spread_sums(b, a):
                for g in range(NG):
                    pool.wait_ge(rsum_ready.sem, rsum_ready.at(b, a * NG + g + 1))
                    if g > 0:
                        pool.wait_ge(rsumt_psum.sem, rsumt_psum.at(b, a * NG + g))
                    settle(pool, pool_passed)
                    nc.gpsimd.tensor_copy(rexp[:, :, :, :], rsum[:, a, g * NT:(g + 1) * NT].unsqueeze(3).to_broadcast([P, NT, G, HP])).then_inc(rexp_ready.sem, 1)
                    pool.wait_ge(oth_ready.sem, oth_ready.at(b, a * NG + g + 1))
                    nc.gpsimd.tensor_tensor(otl[:, g], onm[:, :], oth[:, g].bitcast(F32), ALU.subtract).then_inc(otl_ready.sem, 1)

            root(0, 0, 1)
            pool.wait_ge(xn_ready.sem, xn_ready.at(b, NT))
            for t in range(NT):
                nc.gpsimd.tensor_tensor(x_in[:, t], x_in[:, t], bo[:, :], ALU.add).then_inc(xb_ready.sem, 1)
            for t in range(NT):
                s = t % 2
                pool.wait_ge(root_ready.sem, root_ready.at(b, t + 1))
                y, y2, w = rq[:, s, 0], rq[:, s, 1], rq[:, s, 2]
                chain.link(nc.gpsimd.tensor_tensor(y2, y, y, ALU.mult))
                chain.link(nc.gpsimd.tensor_tensor(w, y2, ssq[:, s], ALU.mult))
                settle(pool, pool_passed)
                chain.link(nc.gpsimd.tensor_scalar(y2, w, -0.5, 1.5, ALU.mult, ALU.add))
                nc.gpsimd.tensor_tensor(rq[:, s, 3], y, y2, ALU.mult).then_inc(rq_ready.sem, 1)
                pool.wait_ge(qn_ready.sem, qn_ready.at(b, t + 1))
                v = qn[:, s].rearrange("p (w h d) -> p w h d", w=2, h=H)
                chain.link(nc.gpsimd.tensor_tensor(v, v, gam[:, :, :].unsqueeze(2).to_broadcast([P, 2, H, D]), ALU.mult))
                nc.gpsimd.tensor_tensor(v, v, bet[:, :, :].unsqueeze(2).to_broadcast([P, 2, H, D]), ALU.add).then_inc(qhat_ready.sem, 1)
            spread_sums(b, 0)
            root(1, 1, 2)
            root(1, 0, 3)
            for n in range(2 * NT):
                pool.wait_ge(rot_ready.sem, rot_ready.at(b, n + 1))
                if n >= 2:
                    pool.wait_ge(ql_ready.sem, ql_ready.at(b, n - 1))
                nc.gpsimd.tensor_tensor(qf[:, n % 2, :, R:DK], ta[:, n % 2], tb[:, n % 2], ALU.add).then_inc(rope_ready.sem, 1)
            spread_sums(b, 1)
            root(2, 0, 4)
            chain.end()

    @block.tensor
    def _(pe):
        mm = nc.tensor.matmul

        pe.wait_ge(raw_loaded, n_raw[0])
        for k in range(KC):
            for h in range(H):
                last = mm(bank[k][:, h * R:(h + 1) * R], r_wqt[:, h, k * P:(k + 1) * P], r_kvbt[:, h], start=True, stop=True)
        for g in range(NG):
            for q in range(G):
                h = g * G + q
                last = mm(bank[2 + g // 2][q * R:(q + 1) * R, (g % 2) * C:(g % 2 + 1) * C], r_kvbt[:, h], r_wob[:, h], start=True, stop=True)
        last.then_inc(folded_psum, 1)
        pe.wait_ge(weights_ready, len(SPLIT))
        pe.wait_ge(va_zeroed, 1)

        def transpose_tokens(b, stage):
            for t in range(NT):
                pe.wait_ge(xn_ready.sem, xn_ready.at(b, stage * NT + t + 1))
                for k in range(KC):
                    ins = nc.tensor.transpose(bank[4 + k][:, t * P:(t + 1) * P], xn[:, t, k * P:(k + 1) * P], ident[:, :])
                    if t == NT - 1:
                        ins.then_inc(xt_psum.sem, 1)

        def hi_split(b, stage):
            pe.wait_ge(xth_ready.sem, xth_ready.at(b, (stage + 1) * KC))

        def lo_split(b, stage):
            pe.wait_ge(xtl_ready.sem, xtl_ready.at(b, (stage + 1) * KC))

        def project_qkv(b, t):
            if t >= 2:
                pe.wait_ge(qn_ready.sem, qn_ready.at(b, t - 1))
                pe.wait_ge(v_ready.sem, v_ready.at(b, t - 1))
            for m, (x_, w_) in enumerate(TERMS):
                if t == 0 and m == 2:
                    lo_split(b, 0)
                for k in range(KC):
                    first, end = m == 0 and k == 0, m == 2 and k == KC - 1
                    tok = XT[x_][:, k, t * P:(t + 1) * P]
                    q = mm(bank[t % 2][:, :], tok, wqkv[:, w_, k, 0:2 * C], start=first, stop=end)
                    v = mm(bank[2 + t % 2][:, 0:C], tok, wqkv[:, w_, k, 2 * C:3 * C], start=first, stop=end)
            q.then_inc(qk_psum.sem, 1)
            v.then_inc(v_psum.sem, 1)

        def transpose_stack(b, t):
            pe.wait_ge(stack_ready.sem, stack_ready.at(b, t + 1))
            for quad in range(4):
                n = 4 * t + quad
                if n >= 4:
                    copied = stackt_dve if quad % 2 else stackt_act
                    pe.wait_ge(copied.sem, copied.at(b, (n - 4) // 2 + 1))
                out = bank[4 + quad].bitcast(BF16)
                for i in range(8):
                    ins = nc.tensor.transpose(out[0:SD, i * P:(i + 1) * P],
                                              stk[:, t % 2, quad * 8 + i].rearrange("p s d -> p (s d)"), ident16[:, :])
                ins.then_inc(stackt_psum.sem, 1)

        def score(b, a, u, pair):
            g, j = u // NT, tile_of(u)
            if u > 0:
                pe.wait_ge(prob_ready.sem, prob_ready.at(b, (a * UNITS + u - 1) * G + 2 * pair + 2))
            n = (j + 1) * P
            for q in (2 * pair, 2 * pair + 1):
                h = g * G + q
                if a == 0:
                    mm(bank[q][:, 0:n], qkt[:, h, j * P:(j + 1) * P], qkt[:, H + h, 0:n], start=True, stop=False)
                else:
                    m = max(n, 2 * P)
                    tok = qt[:, h, j * P:(j + 1) * P]
                    mm(bank[q][:, 0:m], tok, khh[:, 0:m], start=True, stop=False)
                    mm(bank[q][:, 0:m], tok, kll[:, 0:m], start=False, stop=False)
                ins = mm(bank[q][:, n - P:n], ident16[:, :], mask16[:, :], start=False, stop=True)
            ins.then_inc(s_psum.sem, 1)

        def transpose_prob(b, a, u):
            j = tile_of(u)
            pe.wait_ge(prob_ready.sem, prob_ready.at(b, (a * UNITS + u + 1) * G))
            for i in range(j + 1):
                n = first_block(u) + i
                if n >= 2:
                    pe.wait_ge(*block_copied(b, a, n - 2))
                for q in range(G):
                    ins = nc.tensor.transpose(bank[4 + n % 2][:, q * P:(q + 1) * P], prob[:, u % 2, q, i * P:(i + 1) * P], ident[:, :])
                ins.then_inc(probt_psum.sem, 1)

        def weigh_values(b, a, u):
            g, j = u // NT, tile_of(u)
            if u % NT == 0 and g > 0:
                pe.wait_ge(osb_ready.sem, osb_ready.at(b, a * NG + g))
            for i in range(j + 1):
                pe.wait_ge(*block_copied(b, a, first_block(u) + i))
                for q in range(G):
                    val = va[:, i, g * G + q] if a == 0 else vb[:, i]
                    ins = mm(bank[6][q * HP:(q + 1) * HP, j * P:(j + 1) * P], val, probt[:, u % 2, i, q * P:(q + 1) * P],
                             start=i == 0, stop=i == j)
            ins.then_inc(pv_done.sem, 1)

        def transpose_sums(b, a, g):
            pe.wait_ge(rexp_ready.sem, rexp_ready.at(b, a * NG + g + 1))
            if g > 0:
                pe.wait_ge(onm_ready.sem, onm_ready.at(b, a * NG + g))
            for j in range(NT):
                ins = nc.tensor.transpose(bank[7][:, ORDER[j] * P:(ORDER[j] + 1) * P], rexp[:, j].rearrange("p q r -> p (q r)"), ident[:, :])
            ins.then_inc(rsumt_psum.sem, 1)

        def attend(b, a):
            score(b, a, 0, 0)
            score(b, a, 0, 1)
            for u in range(UNITS):
                if u + 1 < UNITS:
                    score(b, a, u + 1, 0)
                if u > 0:
                    weigh_values(b, a, u - 1)
                    if u % NT == 0:
                        transpose_sums(b, a, u // NT - 1)
                if u + 1 < UNITS:
                    score(b, a, u + 1, 1)
                transpose_prob(b, a, u)
            project_out(b, a, 0)
            weigh_values(b, a, UNITS - 1)
            project_out(b, a, 1)
            project_out(b, a, 2)
            transpose_sums(b, a, NG - 1)
            project_out(b, a, NG - 1)

        def project_out(b, a, g):
            w = (woa, wob)[a]
            pe.wait_ge(oth_ready.sem, oth_ready.at(b, a * NG + g + 1))
            pe.wait_ge(otl_ready.sem, otl_ready.at(b, a * NG + g + 1))
            for t in range(NT):
                for m, (x_, w_) in enumerate(TERMS):
                    ins = mm(bank[t][:, 0:C], (oth, otl)[x_][:, g, t * P:(t + 1) * P], w[:, w_, g],
                             start=m == 0 and g == 0, stop=m == 2 and g == NG - 1)
                if g == NG - 1:
                    ins.then_inc(y_psum.sem, 1)

        def project_kv(b):
            for m, (x_, w_) in enumerate(TERMS):
                if m == 2:
                    lo_split(b, 1)
                for k in range(KC):
                    ins = mm(bank[6][0:3 * R, :], wkv[:, w_, k], XT[x_][:, k], start=m == 0 and k == 0, stop=m == 2 and k == KC - 1)
            ins.then_inc(kv_psum.sem, 1)

        def project_q(b, n):
            t, w = divmod(n, 2)
            if n >= 4:
                pe.wait_ge(nope_ready.sem, nope_ready.at(b, n - 3))
                pe.wait_ge(rot_ready.sem, rot_ready.at(b, n - 3))
            for m, (x_, w_) in enumerate(TERMS):
                for k in range(KC):
                    ins = mm(bank[n % 4][:, :], XT[x_][:, k, t * P:(t + 1) * P], wq2[:, w_, k, w * 512:(w + 1) * 512],
                             start=m == 0 and k == 0, stop=m == 2 and k == KC - 1)
            ins.then_inc(q_psum.sem, 1)

        def transpose_q(b, n):
            pe.wait_ge(qh_ready.sem, qh_ready.at(b, n + 1))
            pe.wait_ge(ql_ready.sem, ql_ready.at(b, n + 1))
            for r in range(2):
                m = 2 * n + r
                if m >= 3:
                    copied = qt_dve if (m - 3) % 2 else qt_act
                    pe.wait_ge(copied.sem, copied.at(b, (m - 3) // 2 + 1))
                for i in range(4):
                    ins = nc.tensor.transpose(bank[(4, 5, 7)[m % 3]][:, i * P:(i + 1) * P],
                                              stq[:, n % 2, 4 * r + i].rearrange("p s d -> p (s d)").bitcast(F32), ident[:, :])
                ins.then_inc(qt_psum.sem, 1)

        def gate_up(b, e):
            s = e % 2
            if e == 1:
                pe.wait_ge(logits_ready.sem, logits_ready.at(b, 1))
            if e >= 2:
                pe.wait_ge(hid_ready.sem, hid_ready.at(b, e - 1))
            for w in range(2):
                for m, (x_, w_) in enumerate(TERMS):
                    for k in range(KC):
                        ins = mm(bank[2 * s + w][:, :], wgu[:, w_, e, k, w * I:(w + 1) * I], XT[x_][:, k],
                                 start=m == 0 and k == 0, stop=m == 2 and k == KC - 1)
            ins.then_inc(gate_up_psum.sem, 1)

        def down(b, e):
            s = e % 2
            pe.wait_ge(hidh_ready.sem, hidh_ready.at(b, e + 1))
            pe.wait_ge(hidl_ready.sem, hidl_ready.at(b, e + 1))
            if e >= 2:
                pe.wait_ge(down_added.sem, down_added.at(b, e - 1))
            for t in range(NT):
                for m, (x_, w_) in enumerate(TERMS):
                    ins = mm(bank[4 + 2 * s + t // 2][:, (t % 2) * C:(t % 2 + 1) * C], (hidh, hidl)[x_][:, s, t * P:(t + 1) * P],
                             wd[:, w_, e], start=m == 0, stop=m == 2)
                if t % 2:
                    ins.then_inc(down_psum.sem, 1)

        with pe.Fori(0, NB) as b:
            transpose_tokens(b, 0)
            hi_split(b, 0)
            for t in range(NT):
                project_qkv(b, t)
                if t > 2:
                    transpose_stack(b, t - 3)
            transpose_stack(b, NT - 3)
            transpose_stack(b, NT - 2)
            transpose_stack(b, NT - 1)
            pe.wait_ge(stackt_act.sem, stackt_act.at(b, 2 * NT))
            pe.wait_ge(stackt_dve.sem, stackt_dve.at(b, 2 * NT))
            attend(b, 0)
            transpose_tokens(b, 1)
            hi_split(b, 1)
            project_kv(b)
            for n in range(2 * NT):
                project_q(b, n)
                if n > 1:
                    transpose_q(b, n - 2)
                if n == 2:
                    pe.wait_ge(kf_ready.sem, kf_ready.at(b, 1))
                    settle(pe, pe_passed)
                    for t in range(NT):
                        ins = nc.tensor.transpose(bank[6][:, t * R:(t + 1) * R], kf[0:R, t * P:(t + 1) * P], ident[0:R, 0:R])
                    ins.then_inc(vb_psum.sem, 1)
            transpose_q(b, 2 * NT - 2)
            transpose_q(b, 2 * NT - 1)
            pe.wait_ge(qt_act.sem, qt_act.at(b, 2 * NT))
            pe.wait_ge(qt_dve.sem, qt_dve.at(b, 2 * NT))
            pe.wait_ge(kll_ready.sem, kll_ready.at(b, 1))
            pe.wait_ge(vb_ready.sem, vb_ready.at(b, 1))
            attend(b, 1)
            transpose_tokens(b, 2)
            hi_split(b, 2)
            lo_split(b, 2)
            for t in range(NT):
                for m, (x_, w_) in enumerate(TERMS):
                    for k in range(KC):
                        ins = mm(bank[2][:, t * E:(t + 1) * E], XT[x_][:, k, t * P:(t + 1) * P], wgate[:, w_, k],
                                 start=m == 0 and k == 0, stop=m == 2 and k == KC - 1)
            ins.then_inc(gate_psum.sem, 1)
            gate_up(b, 0)
            for e in range(NE):
                if e + 1 < NE:
                    gate_up(b, e + 1)
                down(b, e)

    @block.scalar
    def _(act):
        chain = Chain(act, act_link, ACT_LINKS)

        def copy(out, in_, **k):
            return nc.scalar.activation(out, in_, ACT.Copy, **k)

        act.wait_ge(raw_loaded, n_raw[0])
        for raw, w, gains in SPLIT:
            if gains:
                act.wait_ge(scaled, gains)
            copy(w[:, 0], raw[tuple([slice(None)] * len(raw.shape))]).then_inc(hi_ready, 1)

        act.preload_act_table_set("natural_log_exp_and_others")

        def split_tokens(b, stage):
            for k in range(KC):
                act.wait_ge(xt_psum.sem, xt_psum.at(b, stage * KC + k + 1))
                copy(xth[:, k], bank[4 + k][:, :]).then_inc(xth_ready.sem, 1)

        def copy_stack(b, t):
            for quad in (0, 2):
                act.wait_ge(stackt_psum.sem, stackt_psum.at(b, 4 * t + quad + 1))
                copy(qkt[:, quad * 8:(quad + 1) * 8, t * P:(t + 1) * P],
                     bank[4 + quad].bitcast(BF16)[0:SD].rearrange("p (h t) -> p h t", h=8)).then_inc(stackt_act.sem, 1)

        def exps(b, a, u, pair):
            j = tile_of(u)
            n = (j + 1) * P
            act.wait_ge(negmax_ready.sem, negmax_ready.at(b, (a * UNITS + u) * 2 + pair + 1))
            if u >= 2:
                act.wait_ge(probt_psum.sem, probt_psum.at(b, a * BLOCKS + first_block(u - 1)))
            for q in (2 * pair, 2 * pair + 1):
                nc.scalar.activation(prob[:, u % 2, q, 0:n], bank[q][:, 0:n], ACT.Exp, bias=negmax[:, a, u, q:q + 1],
                                     accum_out=sums[:, a, u, q:q + 1]).then_inc(prob_ready.sem, 1)

        def copy_block(b, a, u, i):
            n = first_block(u) + i
            act.wait_ge(probt_psum.sem, probt_psum.at(b, a * BLOCKS + n + 1))
            if u >= 2:
                act.wait_ge(pv_done.sem, pv_done.at(b, a * UNITS + u - 1))
            copy(probt[:, u % 2, i], bank[4 + n % 2][:, :]).then_inc(probt_act.sem, 1)

        def copy_out(b, a, g):
            act.wait_ge(pv_done.sem, pv_done.at(b, a * UNITS + (g + 1) * NT))
            if g > 0:
                act.wait_ge(onm_ready.sem, onm_ready.at(b, a * NG + g))
            copy(osb[:, :], bank[6][:, :]).then_inc(osb_ready.sem, 1)

        def split_out(b, a, g):
            act.wait_ge(onm_ready.sem, onm_ready.at(b, a * NG + g + 1))
            copy(oth[:, g], onm[:, :]).then_inc(oth_ready.sem, 1)

        def attend(b, a):
            for u in range(UNITS + 1):
                mine = []
                if u < UNITS:
                    exps(b, a, u, 0)
                if u % NT == 1 and u > NT:
                    copy_out(b, a, u // NT - 1)
                if 0 < u <= UNITS:
                    mine = [i for i in range(tile_of(u - 1) + 1) if acts(first_block(u - 1) + i)]
                if u < UNITS:
                    exps(b, a, u, 1)
                for i in mine:
                    copy_block(b, a, u - 1, i)
                if u % NT == 2 and u > NT:
                    split_out(b, a, u // NT - 1)
            copy_out(b, a, NG - 1)
            split_out(b, a, NG - 1)

        with act.Fori(0, NB) as b:
            chain.start(b)
            split_tokens(b, 0)
            for t in range(NT + 2):
                s = t % 2
                if t < NT:
                    act.wait_ge(qk_psum.sem, qk_psum.at(b, t + 1))
                    if t >= 2:
                        act.wait_ge(ssq_ready.sem, ssq_ready.at(b, t - 1))
                    nc.scalar.activation(sq[:, s], bank[s][:, :], ACT.Square).then_inc(sq_ready.sem, 1)
                    act.wait_ge(v_psum.sem, v_psum.at(b, t + 1))
                    copy(va[:, t, :, 0:D], bank[2 + s][:, 0:C].rearrange("p (h d) -> p h d", h=H)).then_inc(v_ready.sem, 1)
                    act.wait_ge(ssq_ready.sem, ssq_ready.at(b, t + 1))
                    chain.link(nc.scalar.activation(lnv[:, s], ssq[:, s], ACT.Ln))
                    if t >= 2:
                        act.wait_ge(rq_ready.sem, rq_ready.at(b, t - 1))
                    nc.scalar.activation(rq[:, s, 0], lnv[:, s], ACT.Exp, scale=-0.5).then_inc(root_ready.sem, 1)
                if 1 <= t <= NT:
                    s = (t - 1) % 2
                    act.wait_ge(qhat_ready.sem, qhat_ready.at(b, t))
                    if t >= 3:
                        act.wait_ge(stackt_psum.sem, stackt_psum.at(b, 4 * (t - 2)))
                    qv = qn[:, s, 0:C].rearrange("p (h o d) -> p h o d", h=H, o=1)
                    kv = qn[:, s, C:2 * C].rearrange("p (h o d) -> p h o d", h=H, o=1)
                    copy(stk[:, s, 0:H, 0:3], qv.to_broadcast([P, H, 3, D]))
                    copy(stk[:, s, H:2 * H, 0:4:3], kv.to_broadcast([P, H, 2, D]))
                    copy(stk[:, s, H:2 * H, 5], kv[:, :, 0]).then_inc(part1_ready.sem, 1)
                if t >= 2:
                    copy_stack(b, t - 2)
            attend(b, 0)
            split_tokens(b, 1)
            act.wait_ge(kv_psum.sem, kv_psum.at(b, 1))
            copy(kf[0:R], bank[6][0:R]).then_inc(kv_copied.sem, 1)
            for n in range(2 * NT + 3):
                if n >= 3:
                    m = 2 * (n - 3)
                    act.wait_ge(qt_psum.sem, qt_psum.at(b, m + 1))
                    copy(qt[:, 4 * (m % 4):4 * (m % 4) + 4, (m // 4) * P:(m // 4 + 1) * P],
                         bank[(4, 5, 7)[m % 3]].rearrange("p (h t) -> p h t", h=4)).then_inc(qt_act.sem, 1)
                if n < 2 * NT:
                    s = n % 2
                    act.wait_ge(q_psum.sem, q_psum.at(b, n + 1))
                    if n >= 2:
                        act.wait_ge(ql_ready.sem, ql_ready.at(b, n - 1))
                    copy(qf[:, s, :, 0:R], bank[n % 4].rearrange("p (h d) -> p h d", h=8)[:, :, 0:R]).then_inc(nope_ready.sem, 1)
                if n == 1:
                    act.wait_ge(kf_ready.sem, kf_ready.at(b, 1))
                    copy(khh[0:DK], kf[0:DK])
                    copy(khh[DK:2 * DK], kf[0:DK]).then_inc(khh_ready.sem, 1)
                if n == 4:
                    act.wait_ge(vb_psum.sem, vb_psum.at(b, 1))
                    copy(vb[:, :, :], bank[6][:, 0:NT * R].rearrange("p (t r) -> p t r", t=NT)).then_inc(vb_ready.sem, 1)
                if 1 <= n <= 2 * NT:
                    act.wait_ge(rope_ready.sem, rope_ready.at(b, n))
                    act.wait_ge(nope_ready.sem, nope_ready.at(b, n))
                    if n >= 3:
                        act.wait_ge(qt_psum.sem, qt_psum.at(b, 2 * (n - 2)))
                    copy(stq[:, (n - 1) % 2, :, 0], qf[:, (n - 1) % 2]).then_inc(qh_ready.sem, 1)
            attend(b, 1)
            split_tokens(b, 2)
            act.wait_ge(logits_ready.sem, logits_ready.at(b, 1))
            nc.scalar.activation(pexp[:, :, :], lsh[:, :, :], ACT.Exp).then_inc(pexp_ready.sem, 1)
            for e in range(NE):
                s = e % 2
                act.wait_ge(gate_up_psum.sem, gate_up_psum.at(b, e + 1))
                nc.scalar.activation(sg[:, s], bank[2 * s][:, :], ACT.Silu).then_inc(silu_ready.sem, 1)
                act.wait_ge(hid_ready.sem, hid_ready.at(b, e + 1))
                if e >= 2:
                    act.wait_ge(down_psum.sem, down_psum.at(b, 2 * (e - 1)))
                copy(hidh[:, s], hid[:, s]).then_inc(hidh_ready.sem, 1)
            act.preload_act_table_set("natural_log_exp_and_others")
            chain.end()

    @block.vector
    def _(dve):
        chain = Chain(dve, dve_link, DVE_LINKS)
        tt, ts, stt = nc.vector.tensor_tensor, nc.vector.tensor_scalar, nc.vector.scalar_tensor_tensor

        def scale(*ins):
            ins[-1].then_inc(scaled, 1)

        dve.wait_ge(raw_loaded, n_raw[0])
        nc.vector.reduce_sum(r_sum[:, :, :], r_qkv[:, :, 0:2 * C].rearrange("p k (h d) -> p k h d", d=D), axis=AX.X).then_inc(centred, 1)
        dve.wait_ge(centred, 1)
        ts(r_sum[:, :, :], r_sum[:, :, :], 1.0 / D, None, ALU.mult).then_inc(centred, 1)
        dve.wait_ge(centred, 2)
        for k in range(KC):
            v = r_qkv[:, k, 0:2 * C].rearrange("p (h d) -> p h d", d=D)
            ins = tt(v, v, r_sum[:, k].unsqueeze(2).to_broadcast([P, 2 * H, D]), ALU.subtract)
        scale(ins)
        dve.wait_ge(folded_psum, 1)
        for k in range(KC):
            gain = r_ln[:, 0, k:k + 1]
            ts(r_wq2[:, k, :, 0:R], bank[k].rearrange("p (h r) -> p h r", h=H), gain, DK ** -0.5, ALU.mult, ALU.mult)
            ins = ts(r_wq2[:, k, :, R:DK], r_wqr[:, k], gain, DK ** -0.5, ALU.mult, ALU.mult)
        scale(ins)
        for k in range(KC):
            ins = ts(r_kva[:, k, 0:DK], r_kva[:, k, 0:DK], r_ln[:, 0, k:k + 1], None, ALU.mult)
        ins.then_inc(centred, 1)
        dve.wait_ge(centred, 3)
        ts(r_kva[:, :, DK:DK + R:2], r_kva[:, :, R + 1:DK:2], -1.0, None, ALU.mult)
        scale(nc.vector.tensor_copy(r_kva[:, :, DK + 1:DK + R:2], r_kva[:, :, R:DK:2]))
        for g in range(NG):
            ins = nc.vector.tensor_copy(r_wobf[:, g], bank[2 + g // 2][:, (g % 2) * C:(g % 2 + 1) * C])
        scale(ins)
        for k in range(KC):
            ins = ts(r_gu[:, :, k], r_gu[:, :, k], r_ln[:, 1, k:k + 1], None, ALU.mult)
        scale(ins)
        for k in range(KC):
            ins = ts(r_gate[:, k], r_gate[:, k], r_ln[:, 1, k:k + 1], None, ALU.mult)
        scale(ins)
        for n, (raw, w, _) in enumerate(SPLIT):
            dve.wait_ge(hi_ready, n + 1)
            raw_ = raw[tuple([slice(None)] * len(raw.shape))]
            tt(flat(w[:, 1]), flat(raw_), flat(w[:, 0]).bitcast(F32), ALU.subtract).then_inc(weights_ready, 1)

        def tile_stats(stage, src, t):
            return nc.vector.bn_stats(stats[:, stage, t], src[:, t])

        def moments(stage, last):
            chain.link(last)
            settle(dve, dve_passed)
            for t in range(NT):
                ins = nc.vector.bn_aggr(mv[:, stage, t], stats[:, stage, t])
            chain.link(ins)

        def split_tokens(b, stage):
            for k in range(KC):
                dve.wait_ge(xth_ready.sem, xth_ready.at(b, stage * KC + k + 1))
                tt(xtl[:, k], bank[4 + k][:, :], xth[:, k].bitcast(F32), ALU.subtract).then_inc(xtl_ready.sem, 1)

        def copy_stack(b, t):
            for quad in (1, 3):
                dve.wait_ge(stackt_psum.sem, stackt_psum.at(b, 4 * t + quad + 1))
                nc.vector.tensor_copy(qkt[:, quad * 8:(quad + 1) * 8, t * P:(t + 1) * P],
                                      bank[4 + quad].bitcast(BF16)[0:SD].rearrange("p (h t) -> p h t", h=8)).then_inc(stackt_dve.sem, 1)

        def copy_q(b, n):
            m = 2 * n + 1
            dve.wait_ge(qt_psum.sem, qt_psum.at(b, m + 1))
            nc.vector.tensor_copy(qt[:, 4 * (m % 4):4 * (m % 4) + 4, (m // 4) * P:(m // 4 + 1) * P],
                                  bank[(4, 5, 7)[m % 3]].rearrange("p (h t) -> p h t", h=4)).then_inc(qt_dve.sem, 1)

        def maxima(b, a, u, pair):
            n = (tile_of(u) + 1) * P
            dve.wait_ge(s_psum.sem, s_psum.at(b, (a * UNITS + u) * 2 + pair + 1))
            nc.vector.tensor_reduce(negmax[:, a, u, 2 * pair:2 * pair + 2], scores[:, 2 * pair:2 * pair + 2, 0:n], axis=AX.X,
                                    op=ALU.max, negate=True).then_inc(negmax_ready.sem, 1)

        def copy_block(b, a, u, i):
            n = first_block(u) + i
            dve.wait_ge(probt_psum.sem, probt_psum.at(b, a * BLOCKS + n + 1))
            if u >= 2:
                dve.wait_ge(pv_done.sem, pv_done.at(b, a * UNITS + u - 1))
            nc.vector.tensor_copy(probt[:, u % 2, i], bank[4 + n % 2][:, :]).then_inc(probt_dve.sem, 1)

        def invert_sums(b, a, g):
            dve.wait_ge(prob_ready.sem, prob_ready.at(b, (a * UNITS + (g + 1) * NT) * G))
            nc.vector.reciprocal(rsum[:, a, g * NT:(g + 1) * NT], sums[:, a, g * NT:(g + 1) * NT]).then_inc(rsum_ready.sem, 1)

        def normalise_out(b, a, g):
            dve.wait_ge(rsumt_psum.sem, rsumt_psum.at(b, a * NG + g + 1))
            dve.wait_ge(osb_ready.sem, osb_ready.at(b, a * NG + g + 1))
            if g > 0:
                dve.wait_ge(otl_ready.sem, otl_ready.at(b, a * NG + g))
            tt(onm[:, :], bank[7][:, :], osb[:, :], ALU.mult).then_inc(onm_ready.sem, 1)

        def attend(b, a):
            for u in range(UNITS + 1):
                if u < UNITS:
                    maxima(b, a, u, 0)
                mine = []
                if u > 0:
                    mine = [i for i in range(tile_of(u - 1) + 1) if not acts(first_block(u - 1) + i)]
                if u < UNITS:
                    maxima(b, a, u, 1)
                for i in mine:
                    copy_block(b, a, u - 1, i)
                if u > 0 and u % NT == 0:
                    invert_sums(b, a, u // NT - 1)
                if u % NT == 1 and u > NT:
                    normalise_out(b, a, u // NT - 1)
            normalise_out(b, a, NG - 1)

        def add_out(b, a, to, residual):
            for t in range(NT + 1):
                if t < NT:
                    dve.wait_ge(y_psum.sem, y_psum.at(b, a * NT + t + 1))
                    tt(to[:, t], bank[t][:, 0:C], residual[:, t], ALU.add).then_inc(y_added.sem, 1)
                if t > 0:
                    dve.wait_ge(y_added.sem, y_added.at(b, a * NT + t))
                    ins = tile_stats(a + 1, to, t - 1)
            moments(a + 1, ins)

        with dve.Fori(0, NB) as b:
            chain.start(b)
            dve.wait_ge(x_loaded.sem, x_loaded.at(b, 16))
            for t in range(NT):
                ins = tile_stats(0, x_in, t)
            moments(0, ins)
            ts(var[:, 0, 0], mv[:, 0, :, 1], EPS, None, ALU.add).then_inc(var_ready.sem, 1)
            dve.wait_ge(rstd_ready.sem, rstd_ready.at(b, 1))
            for t in range(NT):
                ts(xn[:, t], x_in[:, t], mv[:, 0, t, 0:1], rstd[:, 0, 0, t:t + 1], ALU.subtract, ALU.mult).then_inc(xn_ready.sem, 1)
            split_tokens(b, 0)
            for t in range(NT + 2):
                s = t % 2
                if t < NT:
                    dve.wait_ge(sq_ready.sem, sq_ready.at(b, t + 1))
                    chain.link(nc.vector.reduce_sum(ssq[:, s], sq[:, s].rearrange("p (h d) -> p h d", d=D), axis=AX.X))
                    ts(ssq[:, s], ssq[:, s], 1.0 / D, EPS, ALU.mult, ALU.add).then_inc(ssq_ready.sem, 1)
                    dve.wait_ge(rq_ready.sem, rq_ready.at(b, t + 1))
                    tt(qn[:, s].rearrange("p (h d) -> p h d", d=D), bank[s].rearrange("p (h d) -> p h d", d=D),
                       rq[:, s, 3].unsqueeze(2).to_broadcast([P, 2 * H, D]), ALU.mult).then_inc(qn_ready.sem, 1)
                if t >= 2:
                    copy_stack(b, t - 2)
                if 1 <= t <= NT:
                    s = (t - 1) % 2
                    dve.wait_ge(part1_ready.sem, part1_ready.at(b, t))
                    rv = res1[:, s].rearrange("p (h d) -> p h d", d=D)
                    chain.link(tt(rv, qn[:, s].rearrange("p (h d) -> p h d", d=D), stk[:, s, :, 0], ALU.subtract))
                    nc.vector.tensor_copy(stk[:, s, 0:H, 3:5], rv[:, 0:H].unsqueeze(2).to_broadcast([P, H, 2, D]))
                    chain.link(nc.vector.tensor_copy(stk[:, s, H:2 * H, 1:5:3], rv[:, H:2 * H].unsqueeze(2).to_broadcast([P, H, 2, D])))
                    tt(stk[:, s, 0:H, 5], rv[:, 0:H], stk[:, s, 0:H, 3], ALU.subtract)
                    tt(stk[:, s, H:2 * H, 2], rv[:, H:2 * H], stk[:, s, H:2 * H, 1], ALU.subtract).then_inc(stack_ready.sem, 1)
            attend(b, 0)
            dve.wait_ge(xb_ready.sem, xb_ready.at(b, NT))
            dve.wait_ge(out_stored.sem, out_stored.at(b, 16))
            add_out(b, 0, x1, x_in)
            ts(var[:, 1, 1], mv[:, 1, :, 1], 1.0 + EPS, EPS * EPS, ALU.mult, ALU.add).then_inc(var_ready.sem, 1)
            ts(var[:, 1, 0], mv[:, 1, :, 1], EPS, None, ALU.add).then_inc(var_ready.sem, 1)
            dve.wait_ge(rstd_ready.sem, rstd_ready.at(b, 2))
            for t in range(NT):
                ts(xn[:, t], x1[:, t], mv[:, 1, t, 0:1], rstd[:, 1, 1, t:t + 1], ALU.subtract, ALU.mult).then_inc(xn_ready.sem, 1)
            dve.wait_ge(rstd_ready.sem, rstd_ready.at(b, 3))
            for t in range(NT):
                ts(xp[:, t], x1[:, t], mv[:, 1, t, 0:1], rstd[:, 1, 0, t:t + 1], ALU.subtract, ALU.mult)
            split_tokens(b, 1)
            dve.wait_ge(kv_copied.sem, kv_copied.at(b, 1))
            tt(ka[R:2 * R], bank[6][R:2 * R], coskt[R:2 * R], ALU.mult)
            chain.link(tt(kb[R:2 * R], bank[6][2 * R:3 * R], coskt[2 * R:3 * R], ALU.mult))
            tt(kf[R:2 * R], ka[R:2 * R], kb[R:2 * R], ALU.add).then_inc(kf_ready.sem, 1)
            for n in range(2 * NT + 3):
                if n >= 3:
                    copy_q(b, n - 3)
                if n < 2 * NT:
                    s, t = n % 2, n // 2
                    dve.wait_ge(nope_ready.sem, nope_ready.at(b, n + 1))
                    if n >= 2:
                        dve.wait_ge(rope_ready.sem, rope_ready.at(b, n - 1))
                    qv = bank[n % 4].rearrange("p (h d) -> p h d", h=8)
                    tt(ta[:, s], qv[:, :, R:DK], cosq[:, t:t + 1].to_broadcast([P, 8, R]), ALU.mult)
                    tt(tb[:, s, :, 0:R:2], qv[:, :, R + 1:DK:2], sinq[:, t:t + 1, 0:R:2].to_broadcast([P, 8, R // 2]), ALU.mult)
                    tt(tb[:, s, :, 1:R:2], qv[:, :, R:DK:2], sinq[:, t:t + 1, 1:R:2].to_broadcast([P, 8, R // 2]), ALU.mult).then_inc(rot_ready.sem, 1)
                if n == 2:
                    dve.wait_ge(khh_ready.sem, khh_ready.at(b, 1))
                    tt(kll[0:DK], kf[0:DK], khh[0:DK].bitcast(F32), ALU.subtract)
                    tt(kll[DK:2 * DK], kf[0:DK], khh[0:DK].bitcast(F32), ALU.subtract).then_inc(kll_ready.sem, 1)
                if 1 <= n <= 2 * NT:
                    dve.wait_ge(qh_ready.sem, qh_ready.at(b, n))
                    s = (n - 1) % 2
                    tt(stq[:, s, :, 1], qf[:, s], stq[:, s, :, 0].bitcast(F32), ALU.subtract).then_inc(ql_ready.sem, 1)
            attend(b, 1)
            add_out(b, 1, xp, xp)
            chain.link(tt(var[:, 2, 0], mv[:, 2, :, 0], mv[:, 2, :, 0], ALU.mult))
            stt(var[:, 2, 0], var[:, 2, 0], EPS, mv[:, 2, :, 1], ALU.add, ALU.add).then_inc(var_ready.sem, 1)
            dve.wait_ge(rstd_ready.sem, rstd_ready.at(b, 4))
            for t in range(NT):
                ts(xn[:, t], xp[:, t], rstd[:, 2, 0, t:t + 1], None, ALU.mult).then_inc(xn_ready.sem, 1)
            chain.link(tt(x1[:, :, :], x1[:, :, :], xp[:, :, :], ALU.add))
            split_tokens(b, 2)
            dve.wait_ge(gate_psum.sem, gate_psum.at(b, 1))
            chain.link(tt(lg[:, :, :], bank[2][:, 0:NT * E].rearrange("p (t e) -> p t e", t=NT),
                          ebias[:, :].unsqueeze(1).to_broadcast([P, NT, E]), ALU.add))
            chain.link(nc.vector.tensor_reduce(lmax[:, :], lg[:, :, :], axis=AX.X, op=ALU.max, negate=True))
            tt(lsh[:, :, :], lg[:, :, :], lmax[:, :].unsqueeze(2).to_broadcast([P, NT, E]), ALU.add).then_inc(logits_ready.sem, 1)
            dve.wait_ge(pexp_ready.sem, pexp_ready.at(b, 1))
            other = pexp[:, :, :].unsqueeze(2).to_broadcast([P, NT, E, E])
            own = pexp[:, :, :].unsqueeze(3).to_broadcast([P, NT, E, E])
            tt(cmp1[:, :, :, :], other, own, ALU.is_gt)
            chain.link(tt(cmp2[:, :, :, :], other, own, ALU.is_equal))
            chain.link(tt(cmp2[:, :, :, :], cmp2[:, :, :, :], below[:, :, :].unsqueeze(1).to_broadcast([P, NT, E, E]), ALU.mult))
            chain.link(tt(cmp1[:, :, :, :], cmp1[:, :, :, :], cmp2[:, :, :, :], ALU.add))
            chain.link(nc.vector.reduce_sum(rank[:, :, :], cmp1[:, :, :, :], axis=AX.X))
            chain.link(stt(chosen[:, :, :], rank[:, :, :], 1.5, pexp[:, :, :], ALU.is_lt, ALU.mult))
            chain.link(nc.vector.reduce_sum(den[:, :], chosen[:, :, :], axis=AX.X))
            chain.link(nc.vector.reciprocal(rden[:, :], den[:, :]))
            chain.link(tt(comb[:, :, :], chosen[:, :, :], rden[:, :].unsqueeze(2).to_broadcast([P, NT, E]), ALU.mult))
            for e in range(NE + 1):
                s = e % 2
                if e < NE:
                    dve.wait_ge(silu_ready.sem, silu_ready.at(b, e + 1))
                    tt(hid[:, s], bank[2 * s + 1][:, :], sg[:, s], ALU.mult).then_inc(hid_ready.sem, 1)
                    dve.wait_ge(hidh_ready.sem, hidh_ready.at(b, e + 1))
                    if e >= 2:
                        dve.wait_ge(down_psum.sem, down_psum.at(b, 2 * (e - 1)))
                    tt(hidl[:, s], hid[:, s], hidh[:, s].bitcast(F32), ALU.subtract).then_inc(hidl_ready.sem, 1)
                if e > 0:
                    if e > 1:
                        dve.wait_ge(down_added.sem, down_added.at(b, e - 1))
                    for half in range(2):
                        dve.wait_ge(down_psum.sem, down_psum.at(b, 2 * (e - 1) + half + 1))
                        for t in (2 * half, 2 * half + 1):
                            y = bank[4 + 2 * (1 - s) + half][:, (t % 2) * C:(t % 2 + 1) * C]
                            if e == 1:
                                ins = tt(x1[:, t], y, x1[:, t], ALU.add)
                            else:
                                ins = stt(x1[:, t], y, comb[:, t, e - 2:e - 1], x1[:, t], ALU.mult, ALU.add)
                    ins.then_inc(down_added.sem, 1)
            dve.wait_ge(down_added.sem, down_added.at(b, NE))
            chain.end()


def kernel(**inputs):
    import concourse.bacc as bacc
    from concourse.bass_utils import run_bass_kernel_spmd
    import ml_dtypes

    a = {k[3:]: np.asarray(v) for k, v in inputs.items()}
    f = np.ascontiguousarray
    t = np.arange(L, dtype=np.float32)
    freqs = (np.float32(1.0) / np.power(np.float32(100000.0), np.arange(0, R, 2, dtype=np.float32) / np.float32(R))).astype(np.float32)
    ang = np.outer(t, freqs).astype(np.float32)
    cos, sin = np.repeat(np.cos(ang), 2, axis=1), np.repeat(np.sin(ang), 2, axis=1)
    sign = np.where(np.arange(R) % 2 == 0, -1.0, 1.0).astype(np.float32)
    ones = np.ones((P, P), np.float32)
    arrays = {
        "x_rows": f(a["attn_x"].reshape(NB * L, C)),
        "wq1t": f(a["attn_Wq"].T), "wk1t": f(a["attn_Wk"].T), "wv1t": f(a["attn_Wv"].T), "wo1t": f(a["attn_Wo"].T),
        "gq": a["attn_gq"], "bq": a["attn_bq"], "gk": a["attn_gk"], "bk": a["attn_bk"], "bo": a["attn_bo"],
        "wq2": a["ffn_Wq"],
        "wq2_nope_t": f(a["ffn_Wq"].reshape(C, H, DK)[:, :, :R].transpose(1, 2, 0)),
        "wkva": a["ffn_Wkva"],
        "wkvb_t": f(a["ffn_Wkvb"].reshape(R, H, R).transpose(1, 2, 0)),
        "wo2": a["ffn_Wo"], "w_ln1": a["ffn_w_ln1"], "w_ln2": a["ffn_w_ln2"],
        "wgate": a["ffn_Wgate"], "ebias": a["ffn_expert_bias"],
        "wg": a["ffn_Wg"], "wu": a["ffn_Wu"], "wd": a["ffn_Wd"],
        "swg": a["ffn_sWg"], "swu": a["ffn_sWu"], "swd": a["ffn_sWd"],
        "ident": np.eye(P, dtype=np.float32), "ident16": np.eye(P, dtype=ml_dtypes.bfloat16),
        "mask16": (np.triu(ones, 1) * np.float32(-1e30)).astype(ml_dtypes.bfloat16),
        "below": np.tril(np.ones((E, E), np.float32), -1),
        "cos": f(cos), "sin": f(sin * sign), "cos_t": f(cos.T), "sin_t": f(sin.T),
    }
    nc = bacc.Bacc("TRN2", target_bir_lowering=False, num_devices=1, dynamic_dma_scratch_size=1024)
    dram = {}
    for name, v in arrays.items():
        dram[name] = nc.dram_tensor(f"in_{name}", v.shape, mybir.dt.from_np(v.dtype), kind="ExternalInput").ap()
    dram["x"] = dram["x_rows"].rearrange("(n l) c -> n l c", l=L)
    dram["out"] = nc.dram_tensor("out_rows", (NB * L, C), F32, kind="ExternalOutput").ap()
    build(nc, dram)
    r = run_bass_kernel_spmd(nc, [{f"in_{k}": v for k, v in arrays.items()}], core_ids=[0])
    return r.results[0]["out_rows"].reshape(NB, L, C)
```

```python
from contextlib import ExitStack

import numpy as np

import concourse.bass as bass
from concourse import mybir

F32 = mybir.dt.float32
F32R = mybir.dt.float32r
BF16 = mybir.dt.bfloat16
ALU = mybir.AluOpType
ACT = mybir.ActivationFunctionType
AX = mybir.AxisListType

P = 128
NB, L, C = 16, 512, 256
NT = L // P
KC = C // P
H = 16
D = C // H
HP = 32
G = 4
NG = H // G
M = 1
NM = G // M
SPLITS = 6
SD = SPLITS * D
R = 32
DK = 2 * R
E, I = 8, 128
NE = E + 1
EPS = 1e-5
UNITS = NG * NT
BLOCKS = NG * NT * (NT + 1) // 2

ACT_COPIES = tuple(n in (2, 5, 8) for n in range(NT * (NT + 1) // 2))


def acts(n):
    return ACT_COPIES[n % len(ACT_COPIES)]


def act_count(n):
    return sum(acts(i) for i in range(n))


ACT_BLOCKS = act_count(BLOCKS)
DVE_BLOCKS = BLOCKS - ACT_BLOCKS


ORDER = (0, 1, 2, 3)


def tile_of(u):
    return ORDER[u % NT]


def first_block(u):
    return u // NT * NT * (NT + 1) // 2 + sum(j + 1 for j in ORDER[:u % NT])


class Signal:

    def __init__(self, sem, per_batch, before=0):
        self.sem, self.per_batch, self.before = sem, per_batch, before

    def at(self, b, n):
        return b * self.per_batch + (self.before + n)


def build(nc, t):
    ctx = ExitStack()
    with ctx:
        _build(nc, ctx, t)


def _build(nc, ctx, dram):
    base = (nc.sbuf_base + 63) // 64 * 64
    place = [base]

    def at(name, shape, dt, offset):
        return nc.alloc_sbuf_tensor_at(name, shape, dt, offset=offset)

    def size(shape, dt):
        n = 2 if dt == BF16 else 4
        for s in shape[1:]:
            n *= s
        return (n + 63) // 64 * 64

    def new(name, shape, dt):
        x = at(name, shape, dt, place[0])
        place[0] += size(shape, dt)
        return x

    wqkv = new("wqkv", [P, 2, KC, 3 * C], F32R)
    woa = new("woa", [P, 2, NG, C], F32R)
    wq2 = new("wq2", [P, 2, KC, H * DK], F32R)
    wkv = new("wkv", [P, 2, KC, 3 * R], F32R)
    wob = new("wob", [P, 2, NG, C], F32R)
    wgu = new("wgu", [P, 2, NE, KC, 2 * I], F32R)
    wd = new("wd", [P, 2, NE, C], F32R)
    wgate = new("wgate", [P, 2, KC, E], F32R)
    ident = new("ident", [P, P], F32)
    ident16 = new("ident16", [P, P], BF16)
    mask16 = new("mask16", [P, P], BF16)
    cosq = new("cosq", [P, NT, R], F32)
    sinq = new("sinq", [P, NT, R], F32)
    coskt = new("coskt", [P, L], F32)
    gam = new("gam", [P, 2, D], F32)
    bet = new("bet", [P, 2, D], F32)
    bo = new("bo", [P, C], F32)
    ebias = new("ebias", [P, E], F32)
    below = new("below", [P, E, E], F32)
    expo = new("expo", [P, NT], F32)
    stats = new("stats", [P, 3, NT, 6], F32)
    mv = new("mv", [P, 3, NT, 2], F32)
    var = new("var", [P, 3, 2, NT], F32)
    rstd = new("rstd", [P, 3, 2, NT], F32)
    squares = new("squares", [P, NT], F32)
    ssq = new("ssq", [P, 2, 2 * H], F32)
    lnv = new("lnv", [P, 2, 2 * H], F32)
    rq = new("rq", [P, 2, 4, 2 * H], F32)
    negmax = new("negmax", [P, 2, UNITS, G], F32)
    sums = new("sums", [P, 2, UNITS, G], F32)
    rsum = new("rsum", [P, 2, UNITS, G], F32)
    lg = new("lg", [P, NT, E], F32)
    lmax = new("lmax", [P, NT], F32)
    lsh = new("lsh", [P, NT, E], F32)
    pexp = new("pexp", [P, NT, E], F32)
    cmp1 = new("cmp1", [P, NT, E, E], F32)
    cmp2 = new("cmp2", [P, NT, E, E], F32)
    rank = new("rank", [P, NT, E], F32)
    chosen = new("chosen", [P, NT, E], F32)
    den = new("den", [P, NT], F32)
    rden = new("rden", [P, NT], F32)
    comb = new("comb", [P, NT, E], F32)

    arena = place[0]
    x_in = new("x_in", [P, NT, C], F32)
    x1 = new("x1", [P, NT, C], F32)
    xp = new("xp", [P, NT, C], F32)
    region_x = place[0]
    xn = new("xn", [P, NT, C], F32)
    xth = new("xth", [P, KC, L], F32R)
    xtl = new("xtl", [P, KC, L], F32R)
    place[0] += 4096
    oth = at("oth", [P, NG, L], F32R, region_x)
    otl = at("otl", [P, NG, L], F32R, region_x + 8192)
    region_q = place[0]
    qkt = new("qkt", [SD, 2 * H, L], BF16)
    qt = at("qt", [P, H, L], F32R, region_q)
    sg = at("sg", [P, 2, L], F32, region_q)
    hid = at("hid", [P, 2, L], F32, region_q + 4096)
    hidh = at("hidh", [P, 2, L], F32R, region_q + 8192)
    hidl = at("hidl", [P, 2, L], F32R, region_q + 12288)
    lgt = at("lgt", [P, L], F32, region_q + 16384)
    region_p = place[0]
    prob = new("prob", [P, 2, G, L], F32)
    probt = new("probt", [P, 2, NT, L], F32)
    o = region_p
    sq = at("sq", [P, 2, 2 * C], F32, o)
    qn = at("qn", [P, 2, 2 * C], F32, o + 4096)
    res1 = at("res1", [P, 2, 2 * C], F32, o + 8192)
    stk = at("stk", [P, 2, 2 * H, SPLITS, D], BF16, o + 12288)
    sqs = at("sqs", [P, NT, C], F32, o)
    kf = at("kf", [P, L], F32, o)
    ka = at("ka", [P, L], F32, o + 2048)
    kb = at("kb", [P, L], F32, o + 4096)
    qf = at("qf", [P, 2, 8, DK], F32, o + 8192)
    ta = at("ta", [P, 2, 8, R], F32, o + 12288)
    tb = at("tb", [P, 2, 8, R], F32, o + 14336)
    stq = at("stq", [P, 2, 8, 2, DK], F32R, o + 16384)
    va = new("va", [P, NT, H, HP], F32)
    khh = new("khh", [P, L], F32R)
    kll = new("kll", [P, L], F32R)
    vb = new("vb", [P, NT, R], F32)
    osb = new("osb", [P, L], F32)
    onm = new("onm", [P, L], F32)
    rexp = new("rexp", [P, NT, G, HP], F32)
    assert place[0] <= nc.sbuf_usable_end, place[0]

    place[0] = arena
    r_qkv = new("r_qkv", [P, KC, 3 * C], F32)
    r_woa = new("r_woa", [P, NG, C], F32)
    r_wqt = new("r_wqt", [R, H, C], F32)
    r_wqr = new("r_wqr", [P, KC, H, R], F32)
    r_kvbt = new("r_kvbt", [R, H, R], F32)
    r_wob = new("r_wob", [R, H, C], F32)
    r_wq2 = new("r_wq2", [P, KC, H, DK], F32)
    r_kva = new("r_kva", [P, KC, 3 * R], F32)
    r_wobf = new("r_wobf", [P, NG, C], F32)
    r_gu = new("r_gu", [P, NE, KC, 2 * I], F32)
    r_d = new("r_d", [P, NE, C], F32)
    r_gate = new("r_gate", [P, KC, E], F32)
    r_ln = new("r_ln", [P, 2, KC], F32)
    r_sum = new("r_sum", [P, KC, 2 * H], F32)
    assert place[0] <= nc.sbuf_usable_end, place[0]

    scores = ctx.enter_context(nc.psum_tensor("scores", [P, 4, 512], F32))
    bank = [scores[:, i] for i in range(4)]
    bank += [ctx.enter_context(nc.psum_tensor(f"bank{i}", [P, 512], F32))[:, :] for i in range(4, 8)]

    def sem(name):
        return ctx.enter_context(nc.semaphore(name))

    raw_loaded = sem("raw_loaded")
    zeroed = sem("zeroed")
    va_zeroed = sem("va_zeroed")
    folded_psum = sem("folded_psum")
    centred = sem("centred")
    scaled = sem("scaled")
    hi_ready = sem("hi_ready")
    weights_ready = sem("weights_ready")
    x_loaded = Signal(sem("x_loaded"), 16)
    out_stored = Signal(sem("out_stored"), 16)
    var_ready = Signal(sem("var_ready"), 4)
    rstd_ready = Signal(sem("rstd_ready"), 4)
    xn_ready = Signal(sem("xn_ready"), 3 * NT)
    xt_psum = Signal(sem("xt_psum"), 3 * KC)
    xth_ready = Signal(sem("xth_ready"), 3 * KC)
    xtl_ready = Signal(sem("xtl_ready"), 3 * KC)
    xb_ready = Signal(sem("xb_ready"), NT)
    qk_psum = Signal(sem("qk_psum"), NT)
    v_psum = Signal(sem("v_psum"), NT)
    sq_ready = Signal(sem("sq_ready"), NT)
    v_ready = Signal(sem("v_ready"), NT)
    ssq_ready = Signal(sem("ssq_ready"), NT)
    root_ready = Signal(sem("root_ready"), NT)
    rq_ready = Signal(sem("rq_ready"), NT)
    qn_ready = Signal(sem("qn_ready"), NT)
    qhat_ready = Signal(sem("qhat_ready"), NT)
    part1_ready = Signal(sem("part1_ready"), NT)
    stack_ready = Signal(sem("stack_ready"), NT)
    stackt_psum = Signal(sem("stackt_psum"), 4 * NT)
    stackt_act = Signal(sem("stackt_act"), 2 * NT)
    stackt_dve = Signal(sem("stackt_dve"), 2 * NT)
    kv_psum = Signal(sem("kv_psum"), 1)
    kv_copied = Signal(sem("kv_copied"), 1)
    kf_ready = Signal(sem("kf_ready"), 1)
    khh_ready = Signal(sem("khh_ready"), 1)
    kll_ready = Signal(sem("kll_ready"), 1)
    vb_psum = Signal(sem("vb_psum"), 1)
    vb_ready = Signal(sem("vb_ready"), 1)
    q_psum = Signal(sem("q_psum"), 2 * NT)
    nope_ready = Signal(sem("nope_ready"), 2 * NT)
    rot_ready = Signal(sem("rot_ready"), 2 * NT)
    rope_ready = Signal(sem("rope_ready"), 2 * NT)
    qh_ready = Signal(sem("qh_ready"), 2 * NT)
    ql_ready = Signal(sem("ql_ready"), 2 * NT)
    qt_psum = Signal(sem("qt_psum"), 4 * NT)
    qt_act = Signal(sem("qt_act"), 2 * NT)
    qt_dve = Signal(sem("qt_dve"), 2 * NT)
    s_psum = Signal(sem("s_psum"), 2 * NM * UNITS)
    negmax_ready = Signal(sem("negmax_ready"), 2 * NM * UNITS)
    prob_ready = Signal(sem("prob_ready"), 2 * G * UNITS)
    probt_psum = Signal(sem("probt_psum"), 2 * BLOCKS)
    probt_act = Signal(sem("probt_act"), 2 * ACT_BLOCKS)
    probt_dve = Signal(sem("probt_dve"), 2 * DVE_BLOCKS)
    pv_done = Signal(sem("pv_done"), 2 * UNITS)
    rsum_ready = Signal(sem("rsum_ready"), 2 * NG)
    rexp_ready = Signal(sem("rexp_ready"), 2 * NG)
    rsumt_psum = Signal(sem("rsumt_psum"), 2 * NG)
    osb_ready = Signal(sem("osb_ready"), 2 * NG)
    onm_ready = Signal(sem("onm_ready"), 2 * NG)
    oth_ready = Signal(sem("oth_ready"), 2 * NG)
    otl_ready = Signal(sem("otl_ready"), 2 * NG)
    y_psum = Signal(sem("y_psum"), 2 * NT)
    y_added = Signal(sem("y_added"), 2 * NT)
    squares_ready = Signal(sem("squares_ready"), NT)
    gatet_psum = Signal(sem("gatet_psum"), 1)
    gatet_copied = Signal(sem("gatet_copied"), 1)
    gate_psum = Signal(sem("gate_psum"), 1)
    logits_ready = Signal(sem("logits_ready"), 1)
    pexp_ready = Signal(sem("pexp_ready"), 1)
    gate_up_psum = Signal(sem("gate_up_psum"), NE)
    silu_ready = Signal(sem("silu_ready"), NE)
    hid_ready = Signal(sem("hid_ready"), NE)
    hidh_ready = Signal(sem("hidh_ready"), NE)
    hidl_ready = Signal(sem("hidl_ready"), NE)
    down_psum = Signal(sem("down_psum"), 2 * NE)
    down_added = Signal(sem("down_added"), NE, before=1)
    dve_passed, pe_passed, pool_passed = sem("dve_passed"), sem("pe_passed"), sem("pool_passed")
    dve_link = sem("dve_link")
    pool_link = sem("pool_link")
    act_link = sem("act_link")
    DVE_LINKS, POOL_LINKS, ACT_LINKS = 28, 18, 4

    block = ctx.enter_context(nc.Block())

    def settle(eng, passed):
        eng.sem_inc(passed, 1)

    class Chain:

        def __init__(self, eng, semaphore, per_batch):
            self.eng, self.sem, self.per_batch = eng, semaphore, per_batch
            self.b, self.n, self.before = 0, 0, None

        def start(self, b):
            if self.before is None:
                self.before = self.n
            self.b, self.n = b, 0

        def link(self, ins):
            self.n += 1
            ins.then_inc(self.sem, 1)
            self.eng.wait_ge(self.sem, self.b * self.per_batch + ((self.before or 0) + self.n))

        def end(self, last):
            assert self.n == self.per_batch - (self.before if last else 0), (self.n, self.per_batch)

    def block_copied(b, a, n):
        if acts(n):
            return probt_act.sem, probt_act.at(b, a * ACT_BLOCKS + act_count(n + 1))
        return probt_dve.sem, probt_dve.at(b, a * DVE_BLOCKS + n + 1 - act_count(n + 1))

    XT = (xth, xtl)
    EARLY = (1, 0, 1, 2)
    KV_STEP = 0
    TOKEN_BANK = (2, 4, 4)
    TERMS = ((0, 0), (0, 1), (1, 0))

    SPLIT = ((r_woa, woa, 0), (r_d, wd, 0), (r_qkv, wqkv, 1), (r_wq2, wq2, 2), (r_kva, wkv, 3), (r_wobf, wob, 4),
             (r_gu, wgu, 5), (r_gate, wgate, 6))

    def flat(x):
        s = [f"d{i}" for i in range(len(x.shape) - 1)]
        return x.rearrange(f"p {' '.join(s)} -> p ({' '.join(s)})")

    n_raw = [0]

    @block.sync
    def _(sp):
        def load(dst, src):
            sp.dma_start(dst, src).then_inc(raw_loaded, 16)
            n_raw[0] += 16

        for n, name in enumerate(("wq1t", "wk1t", "wv1t")):
            load(r_qkv[:, :, n * C:(n + 1) * C], dram[name].rearrange("(k p) n -> p k n", p=P))
        load(r_wqt[:, :, :], dram["wq2_nope_t"].rearrange("h j c -> j h c"))
        load(r_kvbt[:, :, :], dram["wkvb_t"].rearrange("h j r -> j h r"))
        for k in range(KC):
            load(r_wqr[:, k], dram["wq2"][k * P:(k + 1) * P].rearrange("p (h d) -> p h d", h=H)[:, :, R:DK])
        load(r_kva[:, :, 0:DK], dram["wkva"].rearrange("(k p) n -> p k n", p=P))
        load(r_wob[:, :, :], dram["wo2"].rearrange("(h d) n -> d h n", h=H)[0:R])
        for name, n in (("w_ln1", 0), ("w_ln2", 1)):
            for k in range(KC):
                load(r_ln[:, n, k:k + 1], dram[name][k * P:(k + 1) * P].rearrange("(p o) -> p o", o=1))
        for n, name in enumerate(("g", "u")):
            for k in range(KC):
                rows = slice(k * P, (k + 1) * P)
                load(r_gu[:, 0, k, n * I:(n + 1) * I], dram["sw" + name][0, rows])
                load(r_gu[:, 1:NE, k, n * I:(n + 1) * I], dram["w" + name][:, rows].rearrange("e p i -> p e i"))
        load(r_d[:, 0], dram["swd"][0])
        load(r_d[:, 1:NE], dram["wd"].rearrange("e i c -> i e c"))
        load(r_gate[:, :, :], dram["wgate"].rearrange("(k p) e -> p k e", p=P))
        load(ident[:, :], dram["ident"])
        load(ident16[:, :], dram["ident16"])
        load(mask16[:, :], dram["mask16"])
        load(below[:, :, :], dram["below"].rearrange("(o e) f -> o e f", o=1).to_broadcast([P, E, E]))
        load(cosq[:, :, :], dram["cos"].rearrange("(t p) r -> p t r", p=P))
        load(sinq[:, :, :], dram["sin"].rearrange("(t p) r -> p t r", p=P))
        load(coskt[R:2 * R], dram["cos_t"])
        load(coskt[2 * R:3 * R], dram["sin_t"])
        for n, (g_, b_) in enumerate((("gq", "bq"), ("gk", "bk"))):
            load(gam[:, n], dram[g_].rearrange("(o d) -> o d", o=1).to_broadcast([P, D]))
            load(bet[:, n], dram[b_].rearrange("(o d) -> o d", o=1).to_broadcast([P, D]))
        load(bo[:, :], dram["bo"].rearrange("(o d) -> o d", o=1).to_broadcast([P, C]))
        load(ebias[:, :], dram["ebias"].rearrange("(o d) -> o d", o=1).to_broadcast([P, E]))
        sp.wait_ge(zeroed, 1)
        for q in range(G):
            load(r_woa[q * HP:q * HP + D],
                 dram["wo1t"].rearrange("(g q d) n -> q d g n", q=G, d=D)[q])

        sp.sem_inc(out_stored.sem, 16)
        sp.wait_ge(weights_ready, len(SPLIT))
        sp.dma_start(x_in[:, :, :], dram["x"][0].rearrange("(t p) c -> p t c", p=P)).then_inc(x_loaded.sem, 16)
        with sp.Fori(0, NB - 1) as b:
            sp.wait_ge(y_added.sem, y_added.at(b, NT))
            sp.dma_start(x_in[:, :, :], dram["x_rows"][bass.ds(b * L + L, L)].rearrange("(t p) c -> p t c", p=P)).then_inc(x_loaded.sem, 16)
            sp.wait_ge(down_added.sem, down_added.at(b, NE))
            sp.dma_start(dram["out"][bass.ds(b * L, L)].rearrange("(t p) c -> p t c", p=P), x1[:, :, :]).then_inc(out_stored.sem, 16)
        sp.wait_ge(down_added.sem, down_added.at(NB - 1, NE))
        sp.dma_start(dram["out"][(NB - 1) * L:NB * L].rearrange("(t p) c -> p t c", p=P), x1[:, :, :]).then_inc(out_stored.sem, 16)
        sp.wait_ge(out_stored.sem, 16 * (NB + 1))

    @block.gpsimd
    def _(pool):
        chain = Chain(pool, pool_link, POOL_LINKS)
        nc.gpsimd.memset(r_woa[:, :, :], 0.0).then_inc(zeroed, 1)
        nc.gpsimd.memset(expo[:, :], -0.5)
        pool.wait_ge(weights_ready, len(SPLIT))
        nc.gpsimd.memset(va[:, :, :, :], 0.0).then_inc(va_zeroed, 1)
        pool.wait_ge(va_zeroed, 1)

        def root(b, stage, n, count):
            pool.wait_ge(var_ready.sem, var_ready.at(b, count))
            nc.gpsimd.tensor_tensor(rstd[:, stage, n], var[:, stage, n], expo[:, :], ALU.pow).then_inc(rstd_ready.sem, 1)

        def spread_sums(b, a):
            for g in range(NG):
                pool.wait_ge(rsum_ready.sem, rsum_ready.at(b, a * NG + g + 1))
                if g > 0:
                    pool.wait_ge(rsumt_psum.sem, rsumt_psum.at(b, a * NG + g))
                settle(pool, pool_passed)
                nc.gpsimd.tensor_copy(rexp[:, :, :, :], rsum[:, a, g * NT:(g + 1) * NT].unsqueeze(3).to_broadcast([P, NT, G, HP])).then_inc(rexp_ready.sem, 1)
                if g == NG - 1:
                    break
                pool.wait_ge(oth_ready.sem, oth_ready.at(b, a * NG + g + 1))
                nc.gpsimd.tensor_tensor(otl[:, g], onm[:, :], oth[:, g].bitcast(F32), ALU.subtract).then_inc(otl_ready.sem, 1)

        root(0, 0, 0, 1)

        def sequence(b, last):
            chain.start(b)
            pool.wait_ge(xn_ready.sem, xn_ready.at(b, NT))
            for t in range(NT):
                nc.gpsimd.tensor_tensor(x_in[:, t], x_in[:, t], bo[:, :], ALU.add).then_inc(xb_ready.sem, 1)
            for t in range(NT):
                s = t % 2
                pool.wait_ge(root_ready.sem, root_ready.at(b, t + 1))
                y, y2, w = rq[:, s, 0], rq[:, s, 1], rq[:, s, 2]
                chain.link(nc.gpsimd.tensor_tensor(y2, y, y, ALU.mult))
                chain.link(nc.gpsimd.tensor_tensor(w, y2, ssq[:, s], ALU.mult))
                settle(pool, pool_passed)
                chain.link(nc.gpsimd.tensor_scalar(y2, w, -0.5, 1.5, ALU.mult, ALU.add))
                if t >= 2:
                    pool.wait_ge(qn_ready.sem, qn_ready.at(b, t - 1))
                nc.gpsimd.tensor_tensor(rq[:, s, 3], y, y2, ALU.mult).then_inc(rq_ready.sem, 1)
                if t == 0:
                    continue
                pool.wait_ge(qn_ready.sem, qn_ready.at(b, t + 1))
                v = qn[:, s].rearrange("p (w h d) -> p w h d", w=2, h=H)
                chain.link(nc.gpsimd.tensor_tensor(v, v, gam[:, :, :].unsqueeze(2).to_broadcast([P, 2, H, D]), ALU.mult))
                nc.gpsimd.tensor_tensor(v, v, bet[:, :, :].unsqueeze(2).to_broadcast([P, 2, H, D]), ALU.add).then_inc(qhat_ready.sem, 1)
            spread_sums(b, 0)
            root(b, 1, 1, 2)
            root(b, 1, 0, 3)
            for n in range(2 * NT):
                pool.wait_ge(rot_ready.sem, rot_ready.at(b, n + 1))
                if n >= 2:
                    pool.wait_ge(ql_ready.sem, ql_ready.at(b, n - 1))
                nc.gpsimd.tensor_tensor(qf[:, n % 2, :, R:DK], ta[:, n % 2], tb[:, n % 2], ALU.add).then_inc(rope_ready.sem, 1)
                if n - KV_STEP in (1, 2, 3, 6, 7):
                    pool.wait_ge(rope_ready.sem, rope_ready.at(b, n + 1))
                if n == KV_STEP + 1:
                    pool.wait_ge(kv_copied.sem, kv_copied.at(b, 1))
                    chain.link(nc.gpsimd.tensor_tensor(ka[R:2 * R], kf[R:2 * R], coskt[R:2 * R], ALU.mult))
                if n == KV_STEP + 2:
                    chain.link(nc.gpsimd.tensor_tensor(kb[R:2 * R], kf[2 * R:3 * R], coskt[2 * R:3 * R], ALU.mult))
                if n == KV_STEP + 3:
                    nc.gpsimd.tensor_tensor(kf[R:2 * R], ka[R:2 * R], kb[R:2 * R], ALU.add).then_inc(kf_ready.sem, 1)
                    pool.wait_ge(kf_ready.sem, kf_ready.at(b, 1))
                if n == KV_STEP + 6:
                    pool.wait_ge(khh_ready.sem, khh_ready.at(b, 1))
                    chain.link(nc.gpsimd.tensor_tensor(kll[0:DK], kf[0:DK], khh[0:DK].bitcast(F32), ALU.subtract))
                if n == KV_STEP + 7:
                    nc.gpsimd.tensor_tensor(kll[DK:2 * DK], kf[0:DK], khh[0:DK].bitcast(F32), ALU.subtract).then_inc(kll_ready.sem, 1)
                    pool.wait_ge(kll_ready.sem, kll_ready.at(b, 1))
            spread_sums(b, 1)
            root(b, 2, 0, 4)
            if not last:
                root(b + 1, 0, 0, 1)
            chain.end(last)

        with pool.Fori(0, NB - 1) as b:
            sequence(b, last=False)
        sequence(NB - 1, last=True)

    @block.tensor
    def _(pe):
        mm = nc.tensor.matmul

        pe.wait_ge(raw_loaded, n_raw[0])
        for k in range(KC):
            for h in range(H):
                last = mm(bank[k][:, h * R:(h + 1) * R], r_wqt[:, h, k * P:(k + 1) * P], r_kvbt[:, h], start=True, stop=True)
        for g in range(NG):
            for q in range(G):
                h = g * G + q
                last = mm(bank[2 + g // 2][q * R:(q + 1) * R, (g % 2) * C:(g % 2 + 1) * C], r_kvbt[:, h], r_wob[:, h], start=True, stop=True)
        last.then_inc(folded_psum, 1)
        pe.wait_ge(weights_ready, len(SPLIT))
        pe.wait_ge(va_zeroed, 1)

        def transpose_tokens(b, stage):
            for t in range(NT):
                pe.wait_ge(xn_ready.sem, xn_ready.at(b, stage * NT + t + 1))
                for k in range(KC):
                    ins = nc.tensor.transpose(bank[TOKEN_BANK[stage] + k][:, t * P:(t + 1) * P], xn[:, t, k * P:(k + 1) * P], ident[:, :])
                    if t == NT - 1:
                        ins.then_inc(xt_psum.sem, 1)

        def hi_split(b, stage):
            pe.wait_ge(xth_ready.sem, xth_ready.at(b, (stage + 1) * KC))

        def lo_split(b, stage):
            pe.wait_ge(xtl_ready.sem, xtl_ready.at(b, (stage + 1) * KC))

        def project_qk(b, t):
            for m, (x_, w_) in enumerate(TERMS):
                if t == 0 and m == 2:
                    lo_split(b, 0)
                for k in range(KC):
                    ins = mm(bank[t][:, :], XT[x_][:, k, t * P:(t + 1) * P], wqkv[:, w_, k, 0:2 * C],
                             start=m == 0 and k == 0, stop=m == 2 and k == KC - 1)
            ins.then_inc(qk_psum.sem, 1)

        def project_v(b, t):
            if t == 0:
                pe.wait_ge(down_added.sem, down_added.at(b, 0))
            for m, (x_, w_) in enumerate(TERMS):
                for k in range(KC):
                    ins = mm(bank[4 + t][:, 0:C], XT[x_][:, k, t * P:(t + 1) * P], wqkv[:, w_, k, 2 * C:3 * C],
                             start=m == 0 and k == 0, stop=m == 2 and k == KC - 1)
            ins.then_inc(v_psum.sem, 1)

        def transpose_stack(b, t):
            pe.wait_ge(stack_ready.sem, stack_ready.at(b, t + 1))
            for quad in range(4):
                n = 4 * t + quad
                if n >= 4:
                    copied = stackt_dve if quad % 2 else stackt_act
                    pe.wait_ge(copied.sem, copied.at(b, (n - 4) // 2 + 1))
                else:
                    pe.wait_ge(v_ready.sem, v_ready.at(b, quad + 1))
                out = bank[4 + quad].bitcast(BF16)
                for i in range(8):
                    ins = nc.tensor.transpose(out[0:SD, i * P:(i + 1) * P],
                                              stk[:, t % 2, quad * 8 + i].rearrange("p s d -> p (s d)"), ident16[:, :])
                ins.then_inc(stackt_psum.sem, 1)

        def score(b, a, u, part):
            g, j = u // NT, tile_of(u)
            n = (j + 1) * P
            for q in range(M * part, M * part + M):
                h = g * G + q
                if u > 0:
                    pe.wait_ge(prob_ready.sem, prob_ready.at(b, (a * UNITS + u - 1) * G + q + 1))
                if a == 0:
                    mm(bank[q][:, 0:n], qkt[:, h, j * P:(j + 1) * P], qkt[:, H + h, 0:n], start=True, stop=False)
                else:
                    m = max(n, 2 * P)
                    tok = qt[:, h, j * P:(j + 1) * P]
                    mm(bank[q][:, 0:m], tok, khh[:, 0:m], start=True, stop=False)
                    mm(bank[q][:, 0:m], tok, kll[:, 0:m], start=False, stop=False)
                ins = mm(bank[q][:, n - P:n], ident16[:, :], mask16[:, :], start=False, stop=True)
            ins.then_inc(s_psum.sem, 1)

        def transpose_prob(b, a, u, blocks):
            if 0 in blocks:
                pe.wait_ge(prob_ready.sem, prob_ready.at(b, (a * UNITS + u + 1) * G))
            for i in blocks:
                n = first_block(u) + i
                if n >= 2:
                    pe.wait_ge(*block_copied(b, a, n - 2))
                for q in range(G):
                    ins = nc.tensor.transpose(bank[4 + n % 2][:, q * P:(q + 1) * P], prob[:, u % 2, q, i * P:(i + 1) * P], ident[:, :])
                ins.then_inc(probt_psum.sem, 1)

        def weigh_values(b, a, u):
            g, j = u // NT, tile_of(u)
            if u % NT == 0 and g > 0:
                pe.wait_ge(osb_ready.sem, osb_ready.at(b, a * NG + g))
            for i in range(j + 1):
                pe.wait_ge(*block_copied(b, a, first_block(u) + i))
                for q in range(G):
                    val = va[:, i, g * G + q] if a == 0 else vb[:, i]
                    ins = mm(bank[6][q * HP:(q + 1) * HP, j * P:(j + 1) * P], val, probt[:, u % 2, i, q * P:(q + 1) * P],
                             start=i == 0, stop=i == j)
            ins.then_inc(pv_done.sem, 1)

        def transpose_sums(b, a, g):
            pe.wait_ge(rexp_ready.sem, rexp_ready.at(b, a * NG + g + 1))
            if g > 0:
                pe.wait_ge(onm_ready.sem, onm_ready.at(b, a * NG + g))
            for j in range(NT):
                ins = nc.tensor.transpose(bank[7][:, ORDER[j] * P:(ORDER[j] + 1) * P], rexp[:, j].rearrange("p q r -> p (q r)"), ident[:, :])
            ins.then_inc(rsumt_psum.sem, 1)

        def attend(b, a):
            for part in range(NM):
                score(b, a, 0, part)
            for u in range(UNITS):
                if u + 1 < UNITS:
                    for part in range(NM):
                        score(b, a, u + 1, part)
                early = EARLY[tile_of(u)]
                transpose_prob(b, a, u, range(early))
                if u > 0:
                    weigh_values(b, a, u - 1)
                    if u % NT == 0:
                        transpose_sums(b, a, u // NT - 1)
                transpose_prob(b, a, u, range(early, tile_of(u) + 1))
            transpose_sums(b, a, NG - 1)
            weigh_values(b, a, UNITS - 1)
            project_out(b, a, range(NG - 2))
            project_out(b, a, range(NG - 2, NG))

        def project_out(b, a, groups):
            w = (woa, wob)[a]
            for t in range(NT):
                for g in groups:
                    if t == 0:
                        pe.wait_ge(oth_ready.sem, oth_ready.at(b, a * NG + g + 1))
                        pe.wait_ge(otl_ready.sem, otl_ready.at(b, a * NG + g + 1))
                    for m, (x_, w_) in enumerate(TERMS):
                        ins = mm(bank[t][:, 0:C], (oth, otl)[x_][:, g, t * P:(t + 1) * P], w[:, w_, g],
                                 start=m == 0 and g == 0, stop=m == 2 and g == NG - 1)
                if g == NG - 1:
                    ins.then_inc(y_psum.sem, 1)

        def project_kv(b):
            for m, (x_, w_) in enumerate(TERMS):
                for k in range(KC):
                    ins = mm(bank[6][0:3 * R, :], wkv[:, w_, k], XT[x_][:, k], start=m == 0 and k == 0, stop=m == 2 and k == KC - 1)
            ins.then_inc(kv_psum.sem, 1)

        def project_q(b, n):
            t, w = divmod(n, 2)
            if n >= 4:
                pe.wait_ge(nope_ready.sem, nope_ready.at(b, n - 3))
                pe.wait_ge(rot_ready.sem, rot_ready.at(b, n - 3))
            for m, (x_, w_) in enumerate(TERMS):
                if n == 0 and m == 2:
                    lo_split(b, 1)
                for k in range(KC):
                    ins = mm(bank[n % 4][:, :], XT[x_][:, k, t * P:(t + 1) * P], wq2[:, w_, k, w * 512:(w + 1) * 512],
                             start=m == 0 and k == 0, stop=m == 2 and k == KC - 1)
            ins.then_inc(q_psum.sem, 1)

        def transpose_q(b, n):
            pe.wait_ge(qh_ready.sem, qh_ready.at(b, n + 1))
            pe.wait_ge(ql_ready.sem, ql_ready.at(b, n + 1))
            for r in range(2):
                m = 2 * n + r
                if m >= 3:
                    copied = qt_dve if (m - 3) % 2 else qt_act
                    pe.wait_ge(copied.sem, copied.at(b, (m - 3) // 2 + 1))
                for i in range(4):
                    ins = nc.tensor.transpose(bank[(4, 5, 7)[m % 3]][:, i * P:(i + 1) * P],
                                              stq[:, n % 2, 4 * r + i].rearrange("p s d -> p (s d)").bitcast(F32), ident[:, :])
                ins.then_inc(qt_psum.sem, 1)

        def gate_up(b, e):
            s = e % 2
            if e == 1:
                pe.wait_ge(logits_ready.sem, logits_ready.at(b, 1))
            if e >= 2:
                pe.wait_ge(hid_ready.sem, hid_ready.at(b, e - 1))
            for w in range(2):
                for m, (x_, w_) in enumerate(TERMS):
                    for k in range(KC):
                        ins = mm(bank[2 * s + w][:, :], wgu[:, w_, e, k, w * I:(w + 1) * I], XT[x_][:, k],
                                 start=m == 0 and k == 0, stop=m == 2 and k == KC - 1)
            ins.then_inc(gate_up_psum.sem, 1)

        def down(b, e):
            s = e % 2
            pe.wait_ge(hidh_ready.sem, hidh_ready.at(b, e + 1))
            pe.wait_ge(hidl_ready.sem, hidl_ready.at(b, e + 1))
            if e >= 2:
                pe.wait_ge(down_added.sem, down_added.at(b, e - 1))
            for t in range(NT):
                for m, (x_, w_) in enumerate(TERMS):
                    ins = mm(bank[4 + 2 * s + t // 2][:, (t % 2) * C:(t % 2 + 1) * C], (hidh, hidl)[x_][:, s, t * P:(t + 1) * P],
                             wd[:, w_, e], start=m == 0, stop=m == 2)
                if t % 2:
                    ins.then_inc(down_psum.sem, 1)

        def sequence(b, last):
            hi_split(b, 0)
            for t in range(NT + 1):
                if t < NT:
                    project_qk(b, t)
                if t > 0:
                    project_v(b, t - 1)
            for t in range(NT):
                transpose_stack(b, t)
            pe.wait_ge(stackt_act.sem, stackt_act.at(b, 2 * NT))
            pe.wait_ge(stackt_dve.sem, stackt_dve.at(b, 2 * NT))
            attend(b, 0)
            transpose_tokens(b, 1)
            hi_split(b, 1)
            for n in range(2 * NT):
                project_q(b, n)
                if n == KV_STEP:
                    project_kv(b)
                if n > 1:
                    transpose_q(b, n - 2)
                if n == KV_STEP + 3:
                    pe.wait_ge(kv_copied.sem, kv_copied.at(b, 1))
                    settle(pe, pe_passed)
                    for t in range(NT):
                        ins = nc.tensor.transpose(bank[6][:, t * R:(t + 1) * R], kf[0:R, t * P:(t + 1) * P], ident[0:R, 0:R])
                    ins.then_inc(vb_psum.sem, 1)
            transpose_q(b, 2 * NT - 2)
            transpose_q(b, 2 * NT - 1)
            pe.wait_ge(qt_act.sem, qt_act.at(b, 2 * NT))
            pe.wait_ge(qt_dve.sem, qt_dve.at(b, 2 * NT))
            pe.wait_ge(kll_ready.sem, kll_ready.at(b, 1))
            pe.wait_ge(vb_ready.sem, vb_ready.at(b, 1))
            attend(b, 1)
            transpose_tokens(b, 2)
            hi_split(b, 2)
            for m, (x_, w_) in enumerate(TERMS):
                if m == 2:
                    lo_split(b, 2)
                for k in range(KC):
                    ins = mm(bank[3][0:E, :], wgate[:, w_, k], XT[x_][:, k], start=m == 0 and k == 0, stop=m == 2 and k == KC - 1)
            ins.then_inc(gatet_psum.sem, 1)
            pe.wait_ge(gatet_copied.sem, gatet_copied.at(b, 1))
            settle(pe, pe_passed)
            for t in range(NT):
                ins = nc.tensor.transpose(bank[2][:, t * E:(t + 1) * E], lgt[0:E, t * P:(t + 1) * P], ident[0:E, 0:E])
            ins.then_inc(gate_psum.sem, 1)
            gate_up(b, 0)
            for e in range(NE):
                if e + 1 < NE:
                    gate_up(b, e + 1)
                elif not last:
                    transpose_tokens(b + 1, 0)
                down(b, e)

        transpose_tokens(0, 0)

        with pe.Fori(0, NB - 1) as b:
            sequence(b, last=False)
        sequence(NB - 1, last=True)

    @block.scalar
    def _(act):
        chain = Chain(act, act_link, ACT_LINKS)

        def copy(out, in_, **k):
            return nc.scalar.activation(out, in_, ACT.Copy, **k)

        act.wait_ge(raw_loaded, n_raw[0])
        for raw, w, gains in SPLIT:
            if gains:
                act.wait_ge(scaled, gains)
            copy(w[:, 0], raw[tuple([slice(None)] * len(raw.shape))]).then_inc(hi_ready, 1)

        act.preload_act_table_set("natural_log_exp_and_others")

        def split_tokens(b, stage):
            for k in range(KC):
                act.wait_ge(xt_psum.sem, xt_psum.at(b, stage * KC + k + 1))
                copy(xth[:, k], bank[TOKEN_BANK[stage] + k][:, :]).then_inc(xth_ready.sem, 1)

        def copy_stack(b, t):
            for quad in (0, 2):
                act.wait_ge(stackt_psum.sem, stackt_psum.at(b, 4 * t + quad + 1))
                copy(qkt[:, quad * 8:(quad + 1) * 8, t * P:(t + 1) * P],
                     bank[4 + quad].bitcast(BF16)[0:SD].rearrange("p (h t) -> p h t", h=8)).then_inc(stackt_act.sem, 1)

        def exps(b, a, u, part):
            j = tile_of(u)
            n = (j + 1) * P
            act.wait_ge(negmax_ready.sem, negmax_ready.at(b, (a * UNITS + u) * NM + part + 1))
            if u >= 2:
                act.wait_ge(probt_psum.sem, probt_psum.at(b, a * BLOCKS + first_block(u - 1)))
            for q in range(M * part, M * part + M):
                nc.scalar.activation(prob[:, u % 2, q, 0:n], bank[q][:, 0:n], ACT.Exp, bias=negmax[:, a, u, q:q + 1],
                                     accum_out=sums[:, a, u, q:q + 1]).then_inc(prob_ready.sem, 1)

        def copy_block(b, a, u, i):
            n = first_block(u) + i
            act.wait_ge(probt_psum.sem, probt_psum.at(b, a * BLOCKS + n + 1))
            if u >= 2:
                act.wait_ge(pv_done.sem, pv_done.at(b, a * UNITS + u - 1))
            copy(probt[:, u % 2, i], bank[4 + n % 2][:, :]).then_inc(probt_act.sem, 1)

        def copy_out(b, a, g):
            act.wait_ge(pv_done.sem, pv_done.at(b, a * UNITS + (g + 1) * NT))
            if g > 0:
                act.wait_ge(onm_ready.sem, onm_ready.at(b, a * NG + g))
            copy(osb[:, :], bank[6][:, :]).then_inc(osb_ready.sem, 1)

        def split_out(b, a, g):
            act.wait_ge(onm_ready.sem, onm_ready.at(b, a * NG + g + 1))
            copy(oth[:, g], onm[:, :]).then_inc(oth_ready.sem, 1)

        def attend(b, a):
            for u in range(UNITS + 1):
                mine = []
                if u < UNITS:
                    for part in range(NM // 2):
                        exps(b, a, u, part)
                if u % NT == 1 and u > NT:
                    copy_out(b, a, u // NT - 1)
                if 0 < u <= UNITS:
                    mine = [i for i in range(tile_of(u - 1) + 1) if acts(first_block(u - 1) + i)]
                if u < UNITS:
                    for part in range(NM // 2, NM):
                        exps(b, a, u, part)
                for i in mine:
                    copy_block(b, a, u - 1, i)
                if u % NT == 2 and u > NT:
                    split_out(b, a, u // NT - 1)
            copy_out(b, a, NG - 1)
            split_out(b, a, NG - 1)

        def sequence(b, last):
            chain.start(b)
            for step in range(NT + 3):
                t = step - 1
                if 0 <= t < NT:
                    s = t % 2
                    act.wait_ge(ssq_ready.sem, ssq_ready.at(b, t + 1))
                    chain.link(nc.scalar.activation(lnv[:, s], ssq[:, s], ACT.Ln))
                    if t >= 2:
                        act.wait_ge(rq_ready.sem, rq_ready.at(b, t - 1))
                    nc.scalar.activation(rq[:, s, 0], lnv[:, s], ACT.Exp, scale=-0.5).then_inc(root_ready.sem, 1)
                t = step
                if t < NT:
                    s = t % 2
                    act.wait_ge(qk_psum.sem, qk_psum.at(b, t + 1))
                    if t >= 2:
                        act.wait_ge(ssq_ready.sem, ssq_ready.at(b, t - 1))
                    nc.scalar.activation(sq[:, s], bank[t][:, :], ACT.Square).then_inc(sq_ready.sem, 1)
                t = step - 1
                if 0 <= t < NT:
                    act.wait_ge(v_psum.sem, v_psum.at(b, t + 1))
                    copy(va[:, t, :, 0:D], bank[4 + t][:, 0:C].rearrange("p (h d) -> p h d", h=H)).then_inc(v_ready.sem, 1)
                t = step - 2
                if 0 <= t < NT:
                    s = t % 2
                    act.wait_ge(qhat_ready.sem, qhat_ready.at(b, t + 1))
                    if t >= 2:
                        act.wait_ge(stackt_psum.sem, stackt_psum.at(b, 4 * (t - 1)))
                    qv = qn[:, s, 0:C].rearrange("p (h o d) -> p h o d", h=H, o=1)
                    kv = qn[:, s, C:2 * C].rearrange("p (h o d) -> p h o d", h=H, o=1)
                    copy(stk[:, s, 0:H, 0:3], qv.to_broadcast([P, H, 3, D]))
                    copy(stk[:, s, H:2 * H, 0:4:3], kv.to_broadcast([P, H, 2, D]))
                    copy(stk[:, s, H:2 * H, 5], kv[:, :, 0]).then_inc(part1_ready.sem, 1)
                if step >= 3:
                    copy_stack(b, step - 3)
            attend(b, 0)
            split_tokens(b, 1)
            for n in range(2 * NT + 3):
                if n >= 3:
                    m = 2 * (n - 3)
                    act.wait_ge(qt_psum.sem, qt_psum.at(b, m + 1))
                    copy(qt[:, 4 * (m % 4):4 * (m % 4) + 4, (m // 4) * P:(m // 4 + 1) * P],
                         bank[(4, 5, 7)[m % 3]].rearrange("p (h t) -> p h t", h=4)).then_inc(qt_act.sem, 1)
                if n < 2 * NT:
                    s = n % 2
                    act.wait_ge(q_psum.sem, q_psum.at(b, n + 1))
                    if n >= 2:
                        act.wait_ge(ql_ready.sem, ql_ready.at(b, n - 1))
                    copy(qf[:, s, :, 0:R], bank[n % 4].rearrange("p (h d) -> p h d", h=8)[:, :, 0:R]).then_inc(nope_ready.sem, 1)
                if 1 <= n <= 2 * NT:
                    act.wait_ge(rope_ready.sem, rope_ready.at(b, n))
                    act.wait_ge(nope_ready.sem, nope_ready.at(b, n))
                    if n >= 3:
                        act.wait_ge(qt_psum.sem, qt_psum.at(b, 2 * (n - 2)))
                    copy(stq[:, (n - 1) % 2, :, 0], qf[:, (n - 1) % 2]).then_inc(qh_ready.sem, 1)
                if n == KV_STEP:
                    act.wait_ge(kv_psum.sem, kv_psum.at(b, 1))
                    copy(kf[0:3 * R], bank[6][0:3 * R]).then_inc(kv_copied.sem, 1)
                if n == KV_STEP + 5:
                    act.wait_ge(kf_ready.sem, kf_ready.at(b, 1))
                    copy(khh[0:DK], kf[0:DK])
                    copy(khh[DK:2 * DK], kf[0:DK]).then_inc(khh_ready.sem, 1)
                if n == KV_STEP + 4:
                    act.wait_ge(vb_psum.sem, vb_psum.at(b, 1))
                    copy(vb[:, :, :], bank[6][:, 0:NT * R].rearrange("p (t r) -> p t r", t=NT)).then_inc(vb_ready.sem, 1)
            attend(b, 1)
            for t in range(NT):
                act.wait_ge(y_added.sem, y_added.at(b, NT + t + 1))
                nc.scalar.activation(sqs[:, t], xp[:, t], ACT.Square, accum_out=squares[:, t:t + 1]).then_inc(squares_ready.sem, 1)
            split_tokens(b, 2)
            act.wait_ge(gatet_psum.sem, gatet_psum.at(b, 1))
            copy(lgt[0:E], bank[3][0:E, :]).then_inc(gatet_copied.sem, 1)
            act.wait_ge(logits_ready.sem, logits_ready.at(b, 1))
            nc.scalar.activation(pexp[:, :, :], lsh[:, :, :], ACT.Exp).then_inc(pexp_ready.sem, 1)
            for e in range(NE):
                s = e % 2
                act.wait_ge(gate_up_psum.sem, gate_up_psum.at(b, e + 1))
                nc.scalar.activation(sg[:, s], bank[2 * s][:, :], ACT.Silu).then_inc(silu_ready.sem, 1)
                act.wait_ge(hid_ready.sem, hid_ready.at(b, e + 1))
                if e >= 2:
                    act.wait_ge(down_psum.sem, down_psum.at(b, 2 * (e - 1)))
                copy(hidh[:, s], hid[:, s]).then_inc(hidh_ready.sem, 1)
            if not last:
                split_tokens(b + 1, 0)
            act.preload_act_table_set("natural_log_exp_and_others")
            chain.end(last)

        split_tokens(0, 0)

        with act.Fori(0, NB - 1) as b:
            sequence(b, last=False)
        sequence(NB - 1, last=True)

    @block.vector
    def _(dve):
        chain = Chain(dve, dve_link, DVE_LINKS)
        tt, ts, stt = nc.vector.tensor_tensor, nc.vector.tensor_scalar, nc.vector.scalar_tensor_tensor

        def scale(*ins):
            ins[-1].then_inc(scaled, 1)

        dve.wait_ge(raw_loaded, n_raw[0])
        nc.vector.reduce_sum(r_sum[:, :, :], r_qkv[:, :, 0:2 * C].rearrange("p k (h d) -> p k h d", d=D), axis=AX.X).then_inc(centred, 1)
        dve.wait_ge(centred, 1)
        ts(r_sum[:, :, :], r_sum[:, :, :], 1.0 / D, None, ALU.mult).then_inc(centred, 1)
        dve.wait_ge(centred, 2)
        for k in range(KC):
            v = r_qkv[:, k, 0:2 * C].rearrange("p (h d) -> p h d", d=D)
            ins = tt(v, v, r_sum[:, k].unsqueeze(2).to_broadcast([P, 2 * H, D]), ALU.subtract)
        scale(ins)
        dve.wait_ge(folded_psum, 1)
        for k in range(KC):
            gain = r_ln[:, 0, k:k + 1]
            ts(r_wq2[:, k, :, 0:R], bank[k].rearrange("p (h r) -> p h r", h=H), gain, DK ** -0.5, ALU.mult, ALU.mult)
            ins = ts(r_wq2[:, k, :, R:DK], r_wqr[:, k], gain, DK ** -0.5, ALU.mult, ALU.mult)
        scale(ins)
        for k in range(KC):
            ins = ts(r_kva[:, k, 0:DK], r_kva[:, k, 0:DK], r_ln[:, 0, k:k + 1], None, ALU.mult)
        ins.then_inc(centred, 1)
        dve.wait_ge(centred, 3)
        ts(r_kva[:, :, DK:DK + R:2], r_kva[:, :, R + 1:DK:2], -1.0, None, ALU.mult)
        scale(nc.vector.tensor_copy(r_kva[:, :, DK + 1:DK + R:2], r_kva[:, :, R:DK:2]))
        for g in range(NG):
            ins = nc.vector.tensor_copy(r_wobf[:, g], bank[2 + g // 2][:, (g % 2) * C:(g % 2 + 1) * C])
        scale(ins)
        for k in range(KC):
            ins = ts(r_gu[:, :, k], r_gu[:, :, k], r_ln[:, 1, k:k + 1], None, ALU.mult)
        scale(ins)
        for k in range(KC):
            ins = ts(r_gate[:, k], r_gate[:, k], r_ln[:, 1, k:k + 1], None, ALU.mult)
        scale(ins)
        for n, (raw, w, _) in enumerate(SPLIT):
            dve.wait_ge(hi_ready, n + 1)
            raw_ = raw[tuple([slice(None)] * len(raw.shape))]
            tt(flat(w[:, 1]), flat(raw_), flat(w[:, 0]).bitcast(F32), ALU.subtract).then_inc(weights_ready, 1)

        def tile_stats(stage, src, t):
            return nc.vector.bn_stats(stats[:, stage, t], src[:, t])

        def moments(stage, last):
            chain.link(last)
            settle(dve, dve_passed)
            for t in range(NT):
                ins = nc.vector.bn_aggr(mv[:, stage, t], stats[:, stage, t])
            chain.link(ins)

        def split_tokens(b, stage):
            for k in range(KC):
                dve.wait_ge(xth_ready.sem, xth_ready.at(b, stage * KC + k + 1))
                tt(xtl[:, k], bank[TOKEN_BANK[stage] + k][:, :], xth[:, k].bitcast(F32), ALU.subtract).then_inc(xtl_ready.sem, 1)

        def copy_stack(b, t):
            for quad in (1, 3):
                dve.wait_ge(stackt_psum.sem, stackt_psum.at(b, 4 * t + quad + 1))
                nc.vector.tensor_copy(qkt[:, quad * 8:(quad + 1) * 8, t * P:(t + 1) * P],
                                      bank[4 + quad].bitcast(BF16)[0:SD].rearrange("p (h t) -> p h t", h=8)).then_inc(stackt_dve.sem, 1)

        def copy_q(b, n):
            m = 2 * n + 1
            dve.wait_ge(qt_psum.sem, qt_psum.at(b, m + 1))
            nc.vector.tensor_copy(qt[:, 4 * (m % 4):4 * (m % 4) + 4, (m // 4) * P:(m // 4 + 1) * P],
                                  bank[(4, 5, 7)[m % 3]].rearrange("p (h t) -> p h t", h=4)).then_inc(qt_dve.sem, 1)

        def maxima(b, a, u, part):
            n = (tile_of(u) + 1) * P
            dve.wait_ge(s_psum.sem, s_psum.at(b, (a * UNITS + u) * NM + part + 1))
            nc.vector.tensor_reduce(negmax[:, a, u, M * part:M * part + M], scores[:, M * part:M * part + M, 0:n], axis=AX.X,
                                    op=ALU.max, negate=True).then_inc(negmax_ready.sem, 1)

        def copy_block(b, a, u, i):
            n = first_block(u) + i
            dve.wait_ge(probt_psum.sem, probt_psum.at(b, a * BLOCKS + n + 1))
            if u >= 2:
                dve.wait_ge(pv_done.sem, pv_done.at(b, a * UNITS + u - 1))
            nc.vector.tensor_copy(probt[:, u % 2, i], bank[4 + n % 2][:, :]).then_inc(probt_dve.sem, 1)

        def invert_sums(b, a, g):
            dve.wait_ge(prob_ready.sem, prob_ready.at(b, (a * UNITS + (g + 1) * NT) * G))
            nc.vector.reciprocal(rsum[:, a, g * NT:(g + 1) * NT], sums[:, a, g * NT:(g + 1) * NT]).then_inc(rsum_ready.sem, 1)

        def normalise_out(b, a, g):
            dve.wait_ge(rsumt_psum.sem, rsumt_psum.at(b, a * NG + g + 1))
            dve.wait_ge(osb_ready.sem, osb_ready.at(b, a * NG + g + 1))
            if g > 0:
                dve.wait_ge(otl_ready.sem, otl_ready.at(b, a * NG + g))
            tt(onm[:, :], bank[7][:, :], osb[:, :], ALU.mult).then_inc(onm_ready.sem, 1)

        def attend(b, a):
            for u in range(UNITS + 1):
                if u < UNITS:
                    for part in range(NM):
                        maxima(b, a, u, part)
                mine = []
                if u > 0:
                    mine = [i for i in range(tile_of(u - 1) + 1) if not acts(first_block(u - 1) + i)]
                if u > 0 and u % NT == 0:
                    invert_sums(b, a, u // NT - 1)
                for i in mine:
                    copy_block(b, a, u - 1, i)
                if u % NT == 1 and u > NT:
                    normalise_out(b, a, u // NT - 1)
            normalise_out(b, a, NG - 1)
            dve.wait_ge(oth_ready.sem, oth_ready.at(b, (a + 1) * NG))
            tt(otl[:, NG - 1], onm[:, :], oth[:, NG - 1].bitcast(F32), ALU.subtract).then_inc(otl_ready.sem, 1)

        def add_out(b, a, to, residual):
            for t in range(NT + 1):
                if t < NT:
                    dve.wait_ge(y_psum.sem, y_psum.at(b, a * NT + t + 1))
                    tt(to[:, t], bank[t][:, 0:C], residual[:, t], ALU.add).then_inc(y_added.sem, 1)
                if a == 0 and t > 0:
                    dve.wait_ge(y_added.sem, y_added.at(b, t))
                    ins = tile_stats(1, to, t - 1)
            if a == 0:
                moments(1, ins)

        def first_stats(b, t):
            if t == 0:
                dve.wait_ge(x_loaded.sem, x_loaded.at(b, 16))
            return tile_stats(0, x_in, t)

        def first_variance(b, ins):
            moments(0, ins)
            ts(var[:, 0, 0], mv[:, 0, :, 1], EPS, None, ALU.add).then_inc(var_ready.sem, 1)

        def first_norm(b, t):
            if t == 0:
                dve.wait_ge(rstd_ready.sem, rstd_ready.at(b, 1))
            ts(xn[:, t], x_in[:, t], mv[:, 0, t, 0:1], rstd[:, 0, 0, t:t + 1], ALU.subtract, ALU.mult).then_inc(xn_ready.sem, 1)

        def sequence(b, last):
            chain.start(b)
            for step in range(NT + 3):
                t = step
                if t < NT:
                    s = t % 2
                    dve.wait_ge(sq_ready.sem, sq_ready.at(b, t + 1))
                    chain.link(nc.vector.reduce_sum(ssq[:, s], sq[:, s].rearrange("p (h d) -> p h d", d=D), axis=AX.X))
                    ts(ssq[:, s], ssq[:, s], 1.0 / D, EPS, ALU.mult, ALU.add).then_inc(ssq_ready.sem, 1)
                t = step - 1
                if 0 <= t < NT:
                    s = t % 2
                    dve.wait_ge(rq_ready.sem, rq_ready.at(b, t + 1))
                    tt(qn[:, s].rearrange("p (h d) -> p h d", d=D), bank[t].rearrange("p (h d) -> p h d", d=D),
                       rq[:, s, 3].unsqueeze(2).to_broadcast([P, 2 * H, D]), ALU.mult).then_inc(qn_ready.sem, 1)
                if t == 0:
                    v = qn[:, s].rearrange("p (w h d) -> p w h d", w=2, h=H)
                    dve.wait_ge(qn_ready.sem, qn_ready.at(b, 1))
                    chain.link(tt(v, v, gam[:, :, :].unsqueeze(2).to_broadcast([P, 2, H, D]), ALU.mult))
                    tt(v, v, bet[:, :, :].unsqueeze(2).to_broadcast([P, 2, H, D]), ALU.add).then_inc(qhat_ready.sem, 1)
                t = step - 2
                if 0 <= t < NT:
                    s = t % 2
                    dve.wait_ge(part1_ready.sem, part1_ready.at(b, t + 1))
                    rv = res1[:, s].rearrange("p (h d) -> p h d", d=D)
                    chain.link(tt(rv, qn[:, s].rearrange("p (h d) -> p h d", d=D), stk[:, s, :, 0], ALU.subtract))
                    nc.vector.tensor_copy(stk[:, s, 0:H, 3:5], rv[:, 0:H].unsqueeze(2).to_broadcast([P, H, 2, D]))
                    chain.link(nc.vector.tensor_copy(stk[:, s, H:2 * H, 1:5:3], rv[:, H:2 * H].unsqueeze(2).to_broadcast([P, H, 2, D])))
                    tt(stk[:, s, 0:H, 5], rv[:, 0:H], stk[:, s, 0:H, 3], ALU.subtract)
                    tt(stk[:, s, H:2 * H, 2], rv[:, H:2 * H], stk[:, s, H:2 * H, 1], ALU.subtract).then_inc(stack_ready.sem, 1)
                if step >= 3:
                    copy_stack(b, step - 3)
            attend(b, 0)
            dve.wait_ge(xb_ready.sem, xb_ready.at(b, NT))
            dve.wait_ge(out_stored.sem, out_stored.at(b, 16))
            add_out(b, 0, x1, x_in)
            ts(var[:, 1, 1], mv[:, 1, :, 1], 1.0 + EPS, EPS * EPS, ALU.mult, ALU.add).then_inc(var_ready.sem, 1)
            ts(var[:, 1, 0], mv[:, 1, :, 1], EPS, None, ALU.add).then_inc(var_ready.sem, 1)
            dve.wait_ge(rstd_ready.sem, rstd_ready.at(b, 2))
            for t in range(NT):
                ts(xn[:, t], x1[:, t], mv[:, 1, t, 0:1], rstd[:, 1, 1, t:t + 1], ALU.subtract, ALU.mult).then_inc(xn_ready.sem, 1)
            dve.wait_ge(rstd_ready.sem, rstd_ready.at(b, 3))
            for t in range(NT):
                ts(xp[:, t], x1[:, t], mv[:, 1, t, 0:1], rstd[:, 1, 0, t:t + 1], ALU.subtract, ALU.mult)
            split_tokens(b, 1)
            for n in range(2 * NT + 3):
                if n >= 3:
                    copy_q(b, n - 3)
                if n < 2 * NT:
                    s, t = n % 2, n // 2
                    dve.wait_ge(nope_ready.sem, nope_ready.at(b, n + 1))
                    if n >= 2:
                        dve.wait_ge(rope_ready.sem, rope_ready.at(b, n - 1))
                    qv = bank[n % 4].rearrange("p (h d) -> p h d", h=8)
                    tt(ta[:, s], qv[:, :, R:DK], cosq[:, t:t + 1].to_broadcast([P, 8, R]), ALU.mult)
                    tt(tb[:, s, :, 0:R:2], qv[:, :, R + 1:DK:2], sinq[:, t:t + 1, 0:R:2].to_broadcast([P, 8, R // 2]), ALU.mult)
                    tt(tb[:, s, :, 1:R:2], qv[:, :, R:DK:2], sinq[:, t:t + 1, 1:R:2].to_broadcast([P, 8, R // 2]), ALU.mult).then_inc(rot_ready.sem, 1)
                if 1 <= n <= 2 * NT:
                    dve.wait_ge(qh_ready.sem, qh_ready.at(b, n))
                    s = (n - 1) % 2
                    tt(stq[:, s, :, 1], qf[:, s], stq[:, s, :, 0].bitcast(F32), ALU.subtract).then_inc(ql_ready.sem, 1)
            attend(b, 1)
            add_out(b, 1, xp, xp)
            dve.wait_ge(squares_ready.sem, squares_ready.at(b, NT))
            ts(var[:, 2, 0], squares[:, :], 1.0 / C, EPS, ALU.mult, ALU.add).then_inc(var_ready.sem, 1)
            dve.wait_ge(rstd_ready.sem, rstd_ready.at(b, 4))
            for t in range(NT):
                ts(xn[:, t], xp[:, t], rstd[:, 2, 0, t:t + 1], None, ALU.mult).then_inc(xn_ready.sem, 1)
            split_tokens(b, 2)
            chain.link(tt(x1[:, :, :], x1[:, :, :], xp[:, :, :], ALU.add))
            dve.wait_ge(gate_psum.sem, gate_psum.at(b, 1))
            chain.link(tt(lg[:, :, :], bank[2][:, 0:NT * E].rearrange("p (t e) -> p t e", t=NT),
                          ebias[:, :].unsqueeze(1).to_broadcast([P, NT, E]), ALU.add))
            chain.link(nc.vector.tensor_reduce(lmax[:, :], lg[:, :, :], axis=AX.X, op=ALU.max, negate=True))
            tt(lsh[:, :, :], lg[:, :, :], lmax[:, :].unsqueeze(2).to_broadcast([P, NT, E]), ALU.add).then_inc(logits_ready.sem, 1)
            dve.wait_ge(pexp_ready.sem, pexp_ready.at(b, 1))
            other = pexp[:, :, :].unsqueeze(2).to_broadcast([P, NT, E, E])
            own = pexp[:, :, :].unsqueeze(3).to_broadcast([P, NT, E, E])
            tt(cmp1[:, :, :, :], other, own, ALU.is_gt)
            chain.link(tt(cmp2[:, :, :, :], other, own, ALU.is_equal))
            chain.link(tt(cmp2[:, :, :, :], cmp2[:, :, :, :], below[:, :, :].unsqueeze(1).to_broadcast([P, NT, E, E]), ALU.mult))
            chain.link(tt(cmp1[:, :, :, :], cmp1[:, :, :, :], cmp2[:, :, :, :], ALU.add))
            chain.link(nc.vector.reduce_sum(rank[:, :, :], cmp1[:, :, :, :], axis=AX.X))
            chain.link(stt(chosen[:, :, :], rank[:, :, :], 1.5, pexp[:, :, :], ALU.is_lt, ALU.mult))
            chain.link(nc.vector.reduce_sum(den[:, :], chosen[:, :, :], axis=AX.X))
            chain.link(nc.vector.reciprocal(rden[:, :], den[:, :]))
            chain.link(tt(comb[:, :, :], chosen[:, :, :], rden[:, :].unsqueeze(2).to_broadcast([P, NT, E]), ALU.mult))
            FIRST = 2
            for e in range(NE + 1):
                s = e % 2
                if e < NE:
                    dve.wait_ge(silu_ready.sem, silu_ready.at(b, e + 1))
                    tt(hid[:, s], bank[2 * s + 1][:, :], sg[:, s], ALU.mult).then_inc(hid_ready.sem, 1)
                    dve.wait_ge(hidh_ready.sem, hidh_ready.at(b, e + 1))
                    if e >= 2:
                        dve.wait_ge(down_psum.sem, down_psum.at(b, 2 * (e - 1)))
                    tt(hidl[:, s], hid[:, s], hidh[:, s].bitcast(F32), ALU.subtract).then_inc(hidl_ready.sem, 1)
                if e > 0:
                    if e > 1:
                        dve.wait_ge(down_added.sem, down_added.at(b, e - 1))
                    for half in range(2):
                        dve.wait_ge(down_psum.sem, down_psum.at(b, 2 * (e - 1) + half + 1))
                        for t in (2 * half, 2 * half + 1):
                            y = bank[4 + 2 * (1 - s) + half][:, (t % 2) * C:(t % 2 + 1) * C]
                            if e == 1:
                                ins = tt(x1[:, t], y, x1[:, t], ALU.add)
                            else:
                                ins = stt(x1[:, t], y, comb[:, t, e - 2:e - 1], x1[:, t], ALU.mult, ALU.add)
                    ins.then_inc(down_added.sem, 1)
                if not last:
                    t = e - FIRST
                    if 0 <= t < NT:
                        ins = first_stats(b + 1, t)
                    if t == NT - 1:
                        first_variance(b + 1, ins)
                    if e == NE - 2:
                        for t in range(NT):
                            first_norm(b + 1, t)
                    if e == NE - 1:
                        split_tokens(b + 1, 0)
            dve.wait_ge(down_added.sem, down_added.at(b, NE))
            chain.end(last)

        dve.sem_inc(down_added.sem, 1)
        for t in range(NT):
            ins = first_stats(0, t)
        first_variance(0, ins)
        for t in range(NT):
            first_norm(0, t)
        split_tokens(0, 0)

        with dve.Fori(0, NB - 1) as b:
            sequence(b, last=False)
        sequence(NB - 1, last=True)


def kernel(**inputs):
    import concourse.bacc as bacc
    from concourse.bass_utils import run_bass_kernel_spmd
    import ml_dtypes

    a = {k[3:]: np.asarray(v) for k, v in inputs.items()}
    f = np.ascontiguousarray
    t = np.arange(L, dtype=np.float32)
    freqs = (np.float32(1.0) / np.power(np.float32(100000.0), np.arange(0, R, 2, dtype=np.float32) / np.float32(R))).astype(np.float32)
    ang = np.outer(t, freqs).astype(np.float32)
    cos, sin = np.repeat(np.cos(ang), 2, axis=1), np.repeat(np.sin(ang), 2, axis=1)
    sign = np.where(np.arange(R) % 2 == 0, -1.0, 1.0).astype(np.float32)
    ones = np.ones((P, P), np.float32)
    arrays = {
        "x_rows": f(a["attn_x"].reshape(NB * L, C)),
        "wq1t": f(a["attn_Wq"].T), "wk1t": f(a["attn_Wk"].T), "wv1t": f(a["attn_Wv"].T), "wo1t": f(a["attn_Wo"].T),
        "gq": a["attn_gq"], "bq": a["attn_bq"], "gk": a["attn_gk"], "bk": a["attn_bk"], "bo": a["attn_bo"],
        "wq2": a["ffn_Wq"],
        "wq2_nope_t": f(a["ffn_Wq"].reshape(C, H, DK)[:, :, :R].transpose(1, 2, 0)),
        "wkva": a["ffn_Wkva"],
        "wkvb_t": f(a["ffn_Wkvb"].reshape(R, H, R).transpose(1, 2, 0)),
        "wo2": a["ffn_Wo"], "w_ln1": a["ffn_w_ln1"], "w_ln2": a["ffn_w_ln2"],
        "wgate": a["ffn_Wgate"], "ebias": a["ffn_expert_bias"],
        "wg": a["ffn_Wg"], "wu": a["ffn_Wu"], "wd": a["ffn_Wd"],
        "swg": a["ffn_sWg"], "swu": a["ffn_sWu"], "swd": a["ffn_sWd"],
        "ident": np.eye(P, dtype=np.float32), "ident16": np.eye(P, dtype=ml_dtypes.bfloat16),
        "mask16": (np.triu(ones, 1) * np.float32(-1e30)).astype(ml_dtypes.bfloat16),
        "below": np.tril(np.ones((E, E), np.float32), -1),
        "cos": f(cos), "sin": f(sin * sign), "cos_t": f(cos.T), "sin_t": f(sin.T),
    }
    nc = bacc.Bacc("TRN2", target_bir_lowering=False, num_devices=1, dynamic_dma_scratch_size=1024)
    dram = {}
    for name, v in arrays.items():
        dram[name] = nc.dram_tensor(f"in_{name}", v.shape, mybir.dt.from_np(v.dtype), kind="ExternalInput").ap()
    dram["x"] = dram["x_rows"].rearrange("(n l) c -> n l c", l=L)
    dram["out"] = nc.dram_tensor("out_rows", (NB * L, C), F32, kind="ExternalOutput").ap()
    build(nc, dram)
    r = run_bass_kernel_spmd(nc, [{f"in_{k}": v for k, v in arrays.items()}], core_ids=[0])
    return r.results[0]["out_rows"].reshape(NB, L, C)
```
